# Optimizing a Trainium2 kernel written in Bass

```python
import numpy as np
import jax
import jax.numpy as jnp

def _softmax(x, axis=-1):
    return jax.nn.softmax(x, axis=axis)

def _gelu(x):
    return jax.nn.gelu(x, approximate=True)

def _silu(x):
    return jax.nn.silu(x)

def _sigmoid(x):
    return jax.nn.sigmoid(x)

def _layernorm(x, axis=-1, eps=1e-05):
    m = jnp.mean(x, axis=axis, keepdims=True)
    v = jnp.var(x, axis=axis, keepdims=True)
    return (x - m) / jnp.sqrt(v + eps)

def _scatter_add(tgt, idx, src, axis=0):
    return tgt.at[idx].add(src)

def _segment_sum(src, seg, n):
    return jax.ops.segment_sum(src, seg, n)
kernel_name = 'mk_recurrent_d1_jaxref_r8_f52d35'

def setup_inputs(seed: int=0):
    np.random.seed(seed)
    _w = jnp.asarray

    def _L0_attn_setup():
        import jax, jax.numpy as jnp
        import numpy as np
        from jax import lax
        H = 512
        DIN = 1024
        N = 16
        K = 4
        R = 32
        B_SZ = 2
        L = 256
        EPS = 1e-06

        def rmsnorm(x, w):
            return x * lax.rsqrt(jnp.mean(x * x, axis=-1, keepdims=True) + EPS) * w

        def _selective_scan(x, dt, A, Bm, Cm):
            xT = jnp.transpose(x, (2, 0, 1))
            dtT = jnp.transpose(dt, (2, 0, 1))
            BT = jnp.transpose(Bm, (2, 0, 1))
            CT = jnp.transpose(Cm, (2, 0, 1))

            def step(h, inp):
                x_t, dt_t, B_t, C_t = inp
                dA = jnp.exp(dt_t[..., None] * A)
                dBx = dt_t[..., None] * B_t[:, None, :] * x_t[..., None]
                h = dA * h + dBx
                y = jnp.einsum('bdn,bn->bd', h, C_t)
                return (h, y)
            h0 = jnp.zeros((x.shape[0], x.shape[1], A.shape[1]), dtype=x.dtype)
            _, ys = lax.scan(step, h0, (xT, dtT, BT, CT))
            return jnp.transpose(ys, (1, 2, 0))
        key = jax.random.key(seed)
        ks = jax.random.split(key, 8)
        hidden_states = jax.random.normal(ks[0], (B_SZ, L, H), dtype=jnp.float32)
        s = 0.02
        in_proj_w = jax.random.normal(ks[1], (H, 2 * DIN), dtype=jnp.float32) * s
        conv_w = jax.random.normal(ks[2], (DIN, K), dtype=jnp.float32) * 0.2
        conv_b = jax.random.normal(ks[3], (DIN,), dtype=jnp.float32) * 0.02
        x_proj_w = jax.random.normal(ks[4], (R + 2 * N, DIN), dtype=jnp.float32) * s
        dt_proj_w = jax.random.normal(ks[5], (DIN, R), dtype=jnp.float32) * s
        dt_bias = jax.random.normal(ks[6], (DIN,), dtype=jnp.float32) * 0.5 - 4.0
        A_log = jnp.log(jnp.broadcast_to(jnp.arange(1, N + 1, dtype=jnp.float32)[None, :], (DIN, N)))
        D_param = jnp.ones((DIN,), dtype=jnp.float32)
        out_proj_w = jax.random.normal(ks[7], (H, DIN), dtype=jnp.float32) * s
        dt_ln_w = jnp.ones((R,), dtype=jnp.float32)
        B_ln_w = jnp.ones((N,), dtype=jnp.float32)
        C_ln_w = jnp.ones((N,), dtype=jnp.float32)
        return dict(hidden_states=hidden_states, in_proj_w=in_proj_w, conv_w=conv_w, conv_b=conv_b, x_proj_w=x_proj_w, dt_proj_w=dt_proj_w, dt_bias=dt_bias, A_log=A_log, D_param=D_param, out_proj_w=out_proj_w, dt_ln_w=dt_ln_w, B_ln_w=B_ln_w, C_ln_w=C_ln_w)
    _L0_attn_in = _L0_attn_setup()

    def _L0_ffn_setup():
        import jax, jax.numpy as jnp
        import numpy as np
        H = 512
        I = 1376
        R = 32
        NLEV = 16
        Q_ZERO = 7.5
        Q_STEP = 0.005
        LR_SCALE = 0.02

        def _qlinear(x, q, scale, A, Bm):
            w = (q.astype(jnp.float32) - Q_ZERO) * (scale * Q_STEP)[:, None]
            y = jnp.einsum('bsh,oh->bso', x, w)
            return y + LR_SCALE * (x @ A @ Bm)
        key = jax.random.key(seed)
        ks = jax.random.split(key, 13)
        B, S = (2, 256)
        inp = {'x': jax.random.normal(ks[0], (B, S, H), jnp.float32), 'gate_q': jax.random.randint(ks[1], (I, H), 0, NLEV, jnp.int32), 'gate_scale': jax.random.uniform(ks[2], (I,), jnp.float32), 'gate_A': jax.random.normal(ks[3], (H, R), jnp.float32), 'gate_B': jax.random.normal(ks[4], (R, I), jnp.float32), 'up_q': jax.random.randint(ks[5], (I, H), 0, NLEV, jnp.int32), 'up_scale': jax.random.uniform(ks[6], (I,), jnp.float32), 'up_A': jax.random.normal(ks[7], (H, R), jnp.float32), 'up_B': jax.random.normal(ks[8], (R, I), jnp.float32), 'down_q': jax.random.randint(ks[9], (H, I), 0, NLEV, jnp.int32), 'down_scale': jax.random.uniform(ks[10], (H,), jnp.float32), 'down_A': jax.random.normal(ks[11], (I, R), jnp.float32), 'down_B': jax.random.normal(ks[12], (R, H), jnp.float32)}
        return inp
    _L0_ffn_in = _L0_ffn_setup()
    _d = {'L0_attn_hidden_states': _L0_attn_in['hidden_states'], 'L0_attn_in_proj_w': _L0_attn_in['in_proj_w'], 'L0_attn_conv_w': _L0_attn_in['conv_w'], 'L0_attn_conv_b': _L0_attn_in['conv_b'], 'L0_attn_x_proj_w': _L0_attn_in['x_proj_w'], 'L0_attn_dt_proj_w': _L0_attn_in['dt_proj_w'], 'L0_attn_dt_bias': _L0_attn_in['dt_bias'], 'L0_attn_A_log': _L0_attn_in['A_log'], 'L0_attn_D_param': _L0_attn_in['D_param'], 'L0_attn_out_proj_w': _L0_attn_in['out_proj_w'], 'L0_attn_dt_ln_w': _L0_attn_in['dt_ln_w'], 'L0_attn_B_ln_w': _L0_attn_in['B_ln_w'], 'L0_attn_C_ln_w': _L0_attn_in['C_ln_w'], 'L0_ffn_gate_q': _L0_ffn_in['gate_q'], 'L0_ffn_gate_scale': _L0_ffn_in['gate_scale'], 'L0_ffn_gate_A': _L0_ffn_in['gate_A'], 'L0_ffn_gate_B': _L0_ffn_in['gate_B'], 'L0_ffn_up_q': _L0_ffn_in['up_q'], 'L0_ffn_up_scale': _L0_ffn_in['up_scale'], 'L0_ffn_up_A': _L0_ffn_in['up_A'], 'L0_ffn_up_B': _L0_ffn_in['up_B'], 'L0_ffn_down_q': _L0_ffn_in['down_q'], 'L0_ffn_down_scale': _L0_ffn_in['down_scale'], 'L0_ffn_down_A': _L0_ffn_in['down_A'], 'L0_ffn_down_B': _L0_ffn_in['down_B']}
    _x0 = _d['L0_attn_hidden_states']
    _d['L0_attn_hidden_states'] = jax.random.normal(jax.random.fold_in(jax.random.key(seed), 1), (2, 1024, 512), dtype=_x0.dtype)
    del _x0
    return _d

def reference(L0_attn_hidden_states, L0_attn_in_proj_w, L0_attn_conv_w, L0_attn_conv_b, L0_attn_x_proj_w, L0_attn_dt_proj_w, L0_attn_dt_bias, L0_attn_A_log, L0_attn_D_param, L0_attn_out_proj_w, L0_attn_dt_ln_w, L0_attn_B_ln_w, L0_attn_C_ln_w, L0_ffn_gate_q, L0_ffn_gate_scale, L0_ffn_gate_A, L0_ffn_gate_B, L0_ffn_up_q, L0_ffn_up_scale, L0_ffn_up_A, L0_ffn_up_B, L0_ffn_down_q, L0_ffn_down_scale, L0_ffn_down_A, L0_ffn_down_B):

    def _L0_attn_ref(hidden_states, in_proj_w, conv_w, conv_b, x_proj_w, dt_proj_w, dt_bias, A_log, D_param, out_proj_w, dt_ln_w, B_ln_w, C_ln_w):
        import jax, jax.numpy as jnp
        import numpy as np
        from jax import lax
        H = 512
        DIN = 1024
        N = 16
        K = 4
        R = 32
        B_SZ = 2
        L = 256
        EPS = 1e-06

        def rmsnorm(x, w):
            return x * lax.rsqrt(jnp.mean(x * x, axis=-1, keepdims=True) + EPS) * w

        def _selective_scan(x, dt, A, Bm, Cm):
            xT = jnp.transpose(x, (2, 0, 1))
            dtT = jnp.transpose(dt, (2, 0, 1))
            BT = jnp.transpose(Bm, (2, 0, 1))
            CT = jnp.transpose(Cm, (2, 0, 1))

            def step(h, inp):
                x_t, dt_t, B_t, C_t = inp
                dA = jnp.exp(dt_t[..., None] * A)
                dBx = dt_t[..., None] * B_t[:, None, :] * x_t[..., None]
                h = dA * h + dBx
                y = jnp.einsum('bdn,bn->bd', h, C_t)
                return (h, y)
            h0 = jnp.zeros((x.shape[0], x.shape[1], A.shape[1]), dtype=x.dtype)
            _, ys = lax.scan(step, h0, (xT, dtT, BT, CT))
            return jnp.transpose(ys, (1, 2, 0))
        proj = hidden_states @ in_proj_w
        x, z = jnp.split(proj, 2, axis=-1)
        x = jnp.transpose(x, (0, 2, 1))
        z = jnp.transpose(z, (0, 2, 1))
        Lq = x.shape[-1]
        xp = jnp.pad(x, ((0, 0), (0, 0), (K - 1, 0)))
        xc = conv_b[None, :, None]
        for k in range(K):
            xc = xc + conv_w[None, :, k:k + 1] * xp[:, :, k:k + Lq]
        xc = jax.nn.silu(xc)
        ssm_p = jnp.einsum('bdl,ed->ble', xc, x_proj_w)
        dt_r = rmsnorm(ssm_p[..., :R], dt_ln_w)
        Bm = rmsnorm(ssm_p[..., R:R + N], B_ln_w)
        Cm = rmsnorm(ssm_p[..., R + N:], C_ln_w)
        dt = jnp.einsum('blr,dr->bdl', dt_r, dt_proj_w)
        dt = jax.nn.softplus(dt + dt_bias[None, :, None])
        A = -jnp.exp(A_log)
        Bm = jnp.transpose(Bm, (0, 2, 1))
        Cm = jnp.transpose(Cm, (0, 2, 1))
        ys = _selective_scan(xc, dt, A, Bm, Cm)
        y = (ys + D_param[None, :, None] * xc) * jax.nn.silu(z)
        return jnp.einsum('bdl,hd->blh', y, out_proj_w)

    def _L0_ffn_ref(x, gate_q, gate_scale, gate_A, gate_B, up_q, up_scale, up_A, up_B, down_q, down_scale, down_A, down_B):
        import jax, jax.numpy as jnp
        import numpy as np
        H = 512
        I = 1376
        R = 32
        NLEV = 16
        Q_ZERO = 7.5
        Q_STEP = 0.005
        LR_SCALE = 0.02

        def _qlinear(x, q, scale, A, Bm):
            w = (q.astype(jnp.float32) - Q_ZERO) * (scale * Q_STEP)[:, None]
            y = jnp.einsum('bsh,oh->bso', x, w)
            return y + LR_SCALE * (x @ A @ Bm)
        g = _qlinear(x, gate_q, gate_scale, gate_A, gate_B)
        u = _qlinear(x, up_q, up_scale, up_A, up_B)
        h = jax.nn.silu(g) * u
        return _qlinear(h, down_q, down_scale, down_A, down_B)
    x = L0_attn_hidden_states
    xn = _layernorm(x, axis=-1)
    s = _L0_attn_ref(xn, L0_attn_in_proj_w, L0_attn_conv_w, L0_attn_conv_b, L0_attn_x_proj_w, L0_attn_dt_proj_w, L0_attn_dt_bias, L0_attn_A_log, L0_attn_D_param, L0_attn_out_proj_w, L0_attn_dt_ln_w, L0_attn_B_ln_w, L0_attn_C_ln_w)
    g = _silu(_L0_ffn_ref(xn, L0_ffn_gate_q, L0_ffn_gate_scale, L0_ffn_gate_A, L0_ffn_gate_B, L0_ffn_up_q, L0_ffn_up_scale, L0_ffn_up_A, L0_ffn_up_B, L0_ffn_down_q, L0_ffn_down_scale, L0_ffn_down_A, L0_ffn_down_B))
    x = x + s * g
    return x

_drawn_inputs = setup_inputs


def setup_inputs(seed=0):
    import zlib

    import numpy as np

    out = dict(_drawn_inputs(seed))
    spreads = {'L0_attn_D_param': (1.0, 0.2),
     'L0_attn_dt_ln_w': (1.0, 0.6),
     'L0_attn_B_ln_w': (1.0, 0.6),
     'L0_attn_C_ln_w': (1.0, 0.6)}
    factors = {'L0_attn_dt_proj_w': 8.0,
     'L0_attn_dt_bias': 3.025,
     'L0_ffn_gate_scale': 4.653,
     'L0_ffn_up_scale': 4.66,
     'L0_ffn_down_scale': 4.518}
    for name, (base, spread) in spreads.items():
        noise = np.random.default_rng([zlib.crc32(name.encode()), seed]).standard_normal(out[name].shape)
        drawn = base * np.exp(spread * noise) if base else spread * noise
        out[name] = jnp.asarray(drawn.astype(out[name].dtype))
    for name, factor in factors.items():
        out[name] = (out[name] * factor).astype(out[name].dtype)
    return out
```

```python
from contextlib import ExitStack

import numpy as np

import concourse.bass as bass
from concourse import mybir

F32 = mybir.dt.float32
I32 = mybir.dt.int32
ALU = mybir.AluOpType
ACT = mybir.ActivationFunctionType
AX = mybir.AxisListType

P = 128
NB, L, H = 2, 1024, 512
D, NS, R, KC = 1024, 16, 32, 4
E = R + 2 * NS
I = 1376
IT = 12
IM = 116
HK, DB, TB = H // P, D // P, L // P
HALVES, DH = 2, DB // 2
CH = L // HALVES
JD = CH // P
LN_EPS, RMS_EPS = 1e-5, 1e-6
Q_ZERO, Q_STEP, LR_SCALE = 7.5, 0.005, 0.02
CW, CB, DTB, DP, AL = 0, KC, KC + 1, KC + 2, KC + 3
NCC = AL + NS

T_ACT = TB + 2
T_DVE = HALVES * NS * TB
A_HALF = 2 * DH
A_USES = DB + HALVES * A_HALF
M_HALF = 2 * IT + JD
M_USES = HALVES * M_HALF + TB


def build(nc, x, w_in, chan, w_x, w_dt, ln_w, w_out, gu_q, gu_s, gu_at, gu_b, dn_q, dn_s, dn_at, dn_b, out):
    ctx = ExitStack()
    with ctx:
        def sb(name, shape, dt=F32):
            return ctx.enter_context(nc.sbuf_tensor(name, shape, dt))

        def sem(name):
            return ctx.enter_context(nc.semaphore(name))

        w_gu = nc.dram_tensor("w_gu_scratch", [IT, P, 2 * HK * IM], F32).ap()
        ss_rows = nc.dram_tensor("ss_rows_scratch", [NB, E, L], F32).ap()
        g_rows = nc.dram_tensor("g_scratch", [NB, L, H], F32).ap()

        xnT = sb("xnT", [P, HK, L])
        xc = sb("xc", [P, DB, L])
        dt = sb("dt", [P, DH, L])
        dtx = sb("dtx", [P, DH, L])
        yT = sb("yT", [P, TB, DH * P])
        hb = sb("hb", [P, 2 * DH, L])
        ub = sb("ub", [P, 2, L])
        bn = sb("bn", [P, 2, L])
        hid = sb("hid", [P, IT, CH])
        w_dn = sb("w_dn", [P, IT, H])
        w_ts = sb("w_ts", [P, 2, 2 * HK * IM])
        th = sb("th", [P, 2, CH])
        ident = sb("ident", [P, P])
        cc = sb("cc", [P, DB, NCC])
        lnw = sb("lnw", [P, E])
        st = sb("st", [P, TB, 6])
        mv = sb("mv", [P, TB, 2])
        rs = sb("rs", [P, TB])
        nm = sb("nm", [P, TB])
        ssm = sb("ssm", [P, TB, E])
        ms = sb("ms", [P, TB, 3])
        tmp = hb
        wx = hb[:, DH, 0:DB * E].rearrange("p (k e) -> p k e", e=E)
        ssT = hb[0:E, DH + 1, :]
        wdt = hb[0:R, DH + 2, 0:D]
        sq = hb[:, DH + 3, 0:TB * E].rearrange("p (a e) -> p a e", e=E)
        xt = hb[:, 0:DH, :].rearrange("p i (s c) -> p (i s) c", c=H)
        gt = hb[:, DH:2 * DH, :].rearrange("p i (s c) -> p (i s) c", c=H)
        w_is = w_ts[:, :, 0:HK * P].rearrange("p t (k j) -> p t k j", k=HK)
        hc = cc[:, :, CW:CB + 1]
        negA = cc[:, :, AL:AL + NS]

        psA = ctx.enter_context(nc.psum_tensor("psA", [P, 2, L], F32))
        psT = ctx.enter_context(nc.psum_tensor("psT", [P, 2, 512], F32))
        psM = ctx.enter_context(nc.psum_tensor("psM", [P, 2, 512], F32))

        s_past = sem("s_past")
        s_const = sem("s_const")
        s_ident = sem("s_ident")
        s_negA = sem("s_negA")
        s_prep = sem("s_prep")
        s_q = [sem("s_q0"), sem("s_q1")]
        s_lr = sem("s_lr")
        s_deq = sem("s_deq")
        s_wst = [sem("s_wst0"), sem("s_wst1")]
        s_x = sem("s_x")
        s_st = sem("s_st")
        s_mv = sem("s_mv")
        s_std = sem("s_std")
        s_rstd = sem("s_rstd")
        s_nm = sem("s_nm")
        s_xn = sem("s_xn")
        s_tact = sem("s_T_act")
        s_tdve = sem("s_T_dve")
        s_tfa = sem("s_Ta_full")
        s_tfd = sem("s_Td_full")
        s_af = sem("s_A_free")
        s_mf = sem("s_M_free")
        s_wi = [sem("s_wi0"), sem("s_wi1")]
        s_in = sem("s_in")
        s_acc = sem("s_acc")
        s_tap = sem("s_tap")
        s_thc = sem("s_thc")
        s_xc = sem("s_xc")
        s_wx = sem("s_wx")
        s_wdt = sem("s_wdt")
        s_xp = sem("s_xp")
        s_xpr = sem("s_xpr")
        s_sq = sem("s_sq")
        s_ms = sem("s_ms")
        s_rms = sem("s_rms")
        s_rinv = sem("s_rinv")
        s_sn1 = sem("s_sn1")
        s_sn = sem("s_sn")
        s_bst = sem("s_bst")
        s_dtp = sem("s_dtp")
        s_dtr = sem("s_dtr")
        s_abs = sem("s_abs")
        s_e = sem("s_e")
        s_w1 = sem("s_w1")
        s_ln = sem("s_ln")
        s_nd = sem("s_nd")
        s_rl = sem("s_rl")
        s_dt = sem("s_dt")
        s_dtx = sem("s_dtx")
        s_yz = sem("s_yz")
        s_B = [sem("s_B0"), sem("s_B1")]
        s_u = sem("s_u")
        s_a = sem("s_a")
        s_scan = sem("s_scan")
        s_wt = [sem("s_wt0"), sem("s_wt1")]
        s_fg = sem("s_fg")
        s_fu = sem("s_fu")
        s_fd = sem("s_fd")
        s_th = sem("s_th")
        s_gst = [sem("s_gst0"), sem("s_gst1")]
        s_yb = sem("s_yb")
        s_thz = sem("s_thz")
        s_y = sem("s_y")
        s_wo = sem("s_wo")
        s_xg = sem("s_xg")
        s_sp = sem("s_sp")
        s_o = sem("s_o")
        s_out = sem("s_out")
        CREDITS = {
            "vector": [(s_tdve, 2), (s_af, 2), (s_mf, 2), (s_deq, 2), (s_xc, 2), (s_scan, 2), (s_y, 1)],
            "scalar": [(s_tact, 2), (s_wst[0], 16), (s_wst[1], 16)],
            "tensor": [(s_in, 2), (s_fu, 2)],
            "gpsimd": [(s_u, 8)],
            "sync": [(s_gst[0], 16), (s_gst[1], 16), (s_out, 16)],
        }

        def t_use(b, j):
            return b * T_ACT + j

        def t_group(b, h, n, tb):
            return b * T_DVE + h * (NS * TB) + n * TB + tb

        def a_use(b, j):
            return b * A_USES + (2 * IT + j)

        def a_half(b, h, j):
            return a_use(b, DB + h * A_HALF + j)

        def m_half(b, h, j):
            return b * M_USES + h * M_HALF + j

        def unit(b, h, n, i):
            return b * (HALVES * NS * DH) + h * NS * DH + n * DH + i

        def ffn(b, h, n):
            return b * (HALVES * IT) + h * IT + n

        def blk(b, h, i):
            return b * DB + h * DH + i

        qs = w_ts[:, :, :].bitcast(I32)
        NCONST = 8
        FIRST = 0

        def b_loads(b, h, pair):
            return b * (16 * HALVES * NS // 2) + (16 * (h * NS // 2 + 1)) + pair * 16

        def give_credits(engine, name):
            for s, n in CREDITS[name]:
                engine.sem_inc(s, n)

        def after_wait(engine):
            engine.sem_inc(s_past, 1)

        block = ctx.enter_context(nc.Block())

        @block.sync
        def _(sp):
            give_credits(sp, "sync")
            scale_gu = dt[:, 0:3, :].rearrange("p a l -> p (a l)")[:, 0:2 * IT * IM]
            scale_dn = dt[:, 3, 0:H]
            at_gu = dtx[0:R, 0, :].rearrange("p (g h) -> p g h", g=2)
            b_gu = yT[0:R, :, :].rearrange("p a l -> p (a l)")[:, 0:2 * IT * IM]
            at_dn = xc[0:R, 0:2, :].rearrange("p a l -> p (a l)")[:, 0:IT * IM]
            b_dn = dtx[0:R, 1, 0:H]
            sp.dma_start(scale_gu, gu_s.to_broadcast([P, 2 * IT * IM])).then_inc(s_const, 16)
            sp.dma_start(at_gu, gu_at).then_inc(s_const, 16)
            sp.dma_start(b_gu, gu_b).then_inc(s_const, 16)
            sp.dma_start(scale_dn, dn_s.to_broadcast([P, H])).then_inc(s_const, 16)
            sp.dma_start(at_dn, dn_at).then_inc(s_const, 16)
            sp.dma_start(b_dn, dn_b).then_inc(s_const, 16)
            sp.dma_start(cc[:, :, :], chan).then_inc(s_const, 16)
            sp.dma_start(lnw[:, :], ln_w.to_broadcast([P, E])).then_inc(s_const, 16)
            with sp.Fori(0, IT // 2) as g:
                for t in range(2):
                    sp.wait_ge(s_deq, 2 * g + t + 1)
                    sp.dma_start(qs[:, t, :], gu_q[2 * g + t]).then_inc(s_q[t], 16)
            with sp.Fori(0, IT // 2) as g:
                for t in range(2):
                    sp.wait_ge(s_deq, 2 * g + (IT + t + 1))
                    sp.dma_start(qs[0:IM, t, 0:H], dn_q[2 * g + t]).then_inc(s_q[t], 16)

            with sp.Fori(0, NB) as b:
                sp.wait_ge(s_lr, 2 * IT)
                sp.wait_ge(s_af, 2 * IT + 2)
                sp.wait_ge(s_y, DB * b + 1)
                sp.dma_start(yT[:, :, :], x[b].rearrange("(a p) h -> p a h", p=P)).then_inc(s_x, 16)
                sp.wait_ge(s_out, b * (TB * 16) + 16)
                sp.dma_start(wx, w_x).then_inc(s_wx, 16)
                sp.dma_start(wdt, w_dt).then_inc(s_wdt, 16)
                with sp.Fori(0, DB // 2) as g:
                    for t in range(2):
                        sp.wait_ge(s_in, b * (2 * DB) + 2 * g + (t + 1))
                        sp.dma_start(w_is[:, t, :, :], w_in[2 * g + t]).then_inc(s_wi[t], 16)
                sp.wait_ge(s_tact, t_use(b, TB + 2) + 2)
                sp.dma_start(ss_rows[b], ssT).then_inc(s_bst, 16)
                sp.wait_ge(s_bst, 16 * b + 16)
                after_wait(sp)

                for h in range(HALVES):
                    def load_b(n, t):
                        sp.wait_ge(s_u, unit(b, h, n, 0) + 4)
                        sp.dma_start(bn[:, t, :], ss_rows[b, bass.ds(n + R, 1), :].to_broadcast([P, L])).then_inc(s_B[t], 16)

                    if h == 0:
                        for t in range(2):
                            sp.wait_ge(s_wst[t], 16 + 16 * IT // 2)
                    sp.wait_ge(s_in, b * (2 * DB) + (DB + h * DH + 2))
                    after_wait(sp)
                    with sp.Fori(0, IT // 2) as g:
                        for t in range(2):
                            load_b(2 * g + t, t)
                            sp.wait_ge(s_fu, ffn(b, h, 2 * g + t) + 1)
                            sp.dma_start(w_ts[:, t, :], w_gu[2 * g + t]).then_inc(s_wt[t], 16)
                    for j in range(JD):
                        load_b(IT + j, j % 2)
                    def load_z(i):
                        sp.wait_ge(s_in, b * (2 * DB) + (DB + h * DH + i + 1))
                        sp.dma_start(w_is[:, i % 2, :, :], w_in[DB + h * DH + i]).then_inc(s_wi[i % 2], 16)

                    sp.wait_ge(s_fu, ffn(b, h, IT) + 2)
                    after_wait(sp)
                    load_z(0)
                    load_z(1)
                    for j in range(JD):
                        sp.wait_ge(s_mf, m_half(b, h, 2 * IT + j) + 3)
                        sp.dma_start(g_rows[b, (h * JD + j) * P:(h * JD + j + 1) * P, :], th[:, j % 2, :]
                                     ).then_inc(s_gst[j % 2], 16)
                    if h == 0:
                        sp.wait_ge(s_tfd, t_group(b, h, NS, 0))
                        sp.dma_start(wdt, w_dt).then_inc(s_wdt, 16)
                        sp.dma_start(ssT[0:R, :], ss_rows[b, 0:R, :]).then_inc(s_wdt, 16)
                    load_z(2)
                    load_z(3)

                sp.wait_ge(s_fd, b * TB + TB)
                sp.dma_start(hid[:, 0:DB, :], w_out).then_inc(s_wo, 16)
                sp.wait_ge(s_y, DB * b + DB + 1)
                after_wait(sp)
                for t in range(2):
                    sp.wait_ge(s_gst[t], b * (16 * TB // 2) + (16 * TB // 2 + 16))
                sp.dma_start(hb[:, 0:DH, :].rearrange("p i (s c) -> p (i s) c", c=H),
                             x[b].rearrange("(a p) h -> p a h", p=P)).then_inc(s_xg, 16)
                sp.dma_start(hb[:, DH:2 * DH, :].rearrange("p i (s c) -> p (i s) c", c=H),
                             g_rows[b].rearrange("(a p) h -> p a h", p=P)).then_inc(s_xg, 16)
                with sp.Fori(0, TB) as tb:
                    sp.wait_ge(s_o, b * TB + tb + 1)
                    sp.dma_start(out[b, bass.ts(tb, P), :], xt[:, tb, :]).then_inc(s_out, 16)
            sp.wait_ge(s_out, NB * TB * 16 + 16)

        @block.gpsimd
        def _(pool):
            give_credits(pool, "gpsimd")
            pool.memset(ident[:, :], 0.0).then_inc(s_ident, 1)
            pool.wait_ge(s_ident, 1)
            pool.affine_select(out=ident[:, :], in_=ident[:, :], compare_op=ALU.not_equal, fill=1.0,
                               base=0, pattern=[[-1, P]], channel_multiplier=1).then_inc(s_ident, 1)
            with pool.Fori(0, NB) as b:
                pool.wait_ge(s_nm, b + 1)
                after_wait(pool)
                for tb in range(TB):
                    pool.tensor_scalar(yT[:, tb, :], yT[:, tb, :], rs[:, tb:tb + 1], nm[:, tb:tb + 1],
                                       ALU.mult, ALU.add).then_inc(s_xn, 1)
                for h in range(HALVES):
                    if h == 0:
                        pool.wait_ge(s_tfa, t_use(b, TB))
                    else:
                        pool.wait_ge(s_yb, blk(b, h, 0))
                    after_wait(pool)
                    pool.memset(yT[:, :, :], 0.0).then_inc(s_yz, 1)
                    for i in range(DH):
                        k = blk(b, h, i)
                        pool.wait_ge(s_ln, k + 1)
                        pool.tensor_tensor(dt[:, i, :], dt[:, i, :], dtx[:, i, :], ALU.add).then_inc(s_rl, 1)
                        pool.wait_ge(s_dt, k + 1)
                        pool.tensor_tensor(dtx[:, i, :], dt[:, i, :], xc[:, h * DH + i, :],
                                           ALU.mult).then_inc(s_dtx, 1)
                    pool.wait_ge(s_dtx, blk(b, h, DH))
                    after_wait(pool)

                    def inputs(n, pair, t):
                        pool.wait_ge(s_B[t], b_loads(b, h, pair))
                        for i in range(DH):
                            pool.wait_ge(s_scan, unit(b, h, n, i) + 1)
                            pool.tensor_tensor(ub[:, i % 2, :], dtx[:, i, :], bn[:, t, :], ALU.mult).then_inc(s_u, 1)

                    with pool.Fori(0, NS // 2) as g:
                        for t in range(2):
                            inputs(2 * g + t, g, t)
                pool.wait_ge(s_xg, 32 * b + 32)
                after_wait(pool)
                with pool.Fori(0, TB) as tb:
                    pool.wait_ge(s_mf, m_half(b, HALVES, 0) + tb + 3)
                    pool.tensor_tensor(xt[:, tb, :], xt[:, tb, :], gt[:, tb, :], ALU.add).then_inc(s_o, 1)

        @block.scalar
        def _(act):
            give_credits(act, "scalar")
            act.wait_ge(s_const, 16 * NCONST)
            act.activation(negA, negA, ACT.Exp).then_inc(s_negA, 1)
            with act.Fori(0, IT // 2) as g:
                for t in range(2):
                    act.wait_ge(s_af, 2 * g + (t + 3))
                    act.dma_start(w_gu[2 * g + t], tmp[:, t, 0:2 * HK * IM]).then_inc(s_wst[t], 16)
            for t in range(2):
                act.wait_ge(s_wst[t], 16 + 16 * IT // 2)
            after_wait(act)
            with act.Fori(0, NB) as b:
                act.wait_ge(s_mv, b * TB + TB)
                act.activation(rs[:, :], mv[:, :, 1], ACT.Sqrt, bias=LN_EPS).then_inc(s_std, 1)
                for tb in range(TB):
                    act.wait_ge(s_tfa, t_use(b, tb) + 1)
                    act.activation(xnT[:, :, tb * P:(tb + 1) * P],
                                   psT[:, tb % 2, :].rearrange("p (k t) -> p k t", k=HK),
                                   ACT.Copy).then_inc(s_tact, 1)
                act.wait_ge(s_prep, 2)
                act.wait_ge(s_out, b * (TB * 16) + 16)
                after_wait(act)
                with act.Fori(0, DB // 2) as g:
                    for t in range(2):
                        m = 2 * g + t
                        act.wait_ge(s_in, b * (2 * DB) + m + 3)
                        act.wait_ge(s_xc, b * DB + m + 1)
                        act.activation(tmp[:, t, :], psA[:, t, :], ACT.Identity,
                                       bias=hc[:, m, KC:KC + 1], scale=hc[:, m, KC - 1:KC]).then_inc(s_acc, 1)
                        act.wait_ge(s_af, a_use(b, m) + 3)
                        act.activation(tmp[:, 2 + t, :], tmp[:, t, :], ACT.Tanh).then_inc(s_thc, 1)
                for t in range(2):
                    v = psM[:, t, 0:TB // 2 * E].rearrange("p (a e) -> p a e", e=E)
                    act.wait_ge(s_xp, 2 * b + t + 1)
                    act.activation(sq[:, t * TB // 2:(t + 1) * TB // 2, :], v, ACT.Square).then_inc(s_sq, 1)
                    act.activation(ssm[:, t * TB // 2:(t + 1) * TB // 2, :], v, ACT.Copy).then_inc(s_xpr, 1)
                act.wait_ge(s_ms, 2 * b + 2)
                act.activation(ms[:, :, 0:1], ms[:, :, 0:1], ACT.Sqrt, bias=RMS_EPS, scale=1.0 / R).then_inc(s_rms, 1)
                act.activation(ms[:, :, 1:3], ms[:, :, 1:3], ACT.Sqrt, bias=RMS_EPS, scale=1.0 / NS).then_inc(s_rms, 1)
                for t in range(2):
                    act.wait_ge(s_tfa, t_use(b, TB + t) + 1)
                    act.activation(ssT[:, t * 512:(t + 1) * 512], psT[0:E, t, :], ACT.Copy).then_inc(s_tact, 1)

                for h in range(HALVES):
                    for i in range(DH):
                        k = blk(b, h, i)
                        t = 2 * (i % 2)
                        bias = cc[:, h * DH + i, DTB:DTB + 1]
                        act.wait_ge(s_dtp, k + 1)
                        if i >= 2:
                            act.wait_ge(s_dt, k - 1)
                        elif h:
                            act.wait_ge(s_y, k)
                        act.activation(tmp[:, t, :], psA[:, i % 2, :], ACT.Abs, bias=bias).then_inc(s_abs, 1)
                        act.activation(dt[:, i, :], psA[:, i % 2, :], ACT.Relu, bias=bias).then_inc(s_dtr, 1)
                        act.wait_ge(s_abs, k + 1)
                        act.activation(tmp[:, t, :], tmp[:, t, :], ACT.Exp, scale=-1.0).then_inc(s_e, 1)
                        act.wait_ge(s_e, k + 1)
                        act.activation(tmp[:, t + 1, :], tmp[:, t, :], ACT.Identity, bias=1.0).then_inc(s_w1, 1)
                        act.wait_ge(s_w1, k + 1)
                        act.activation(dtx[:, i, :], tmp[:, t + 1, :], ACT.Ln).then_inc(s_ln, 1)

                    def decay(n, i):
                        act.wait_ge(s_scan, unit(b, h, n, i) + 1)
                        act.activation(psA[:, i % 2, :], dt[:, i, :], ACT.Exp,
                                       scale=negA[:, h * DH + i, bass.ds(n, 1)]).then_inc(s_a, 1)

                    def tanh_gate(n, t):
                        act.wait_ge(s_fg, ffn(b, h, n) + 1)
                        act.activation(th[0:IM, t, :], psM[0:IM, 0, :], ACT.Tanh, scale=0.5).then_inc(s_th, 1)

                    def tanh_down(j):
                        act.wait_ge(s_fd, b * TB + h * JD + j + 1)
                        if j < 2:
                            act.wait_ge(s_mf, m_half(b, h, 2 * (IT - 2 + j) + 1) + 3)
                        else:
                            act.wait_ge(s_gst[j % 2], b * (16 * TB // 2) + 16 * (h * JD // 2 + j // 2 + 1))
                        act.activation(th[:, j % 2, :], psM[:, j % 2, :], ACT.Tanh, scale=0.5).then_inc(s_th, 1)

                    act.wait_ge(s_dt, blk(b, h, DH))
                    for t in range(2):
                        act.wait_ge(s_gst[t], b * (16 * TB // 2) + 16 * (h * JD // 2 + 1))
                    for i in range(DH):
                        decay(0, i)
                    with act.Fori(0, IT // 2) as g:
                        for t in range(2):
                            n = 2 * g + t
                            for i in range(DH):
                                decay(n + 1, i)
                                if i == 2:
                                    tanh_gate(n, t)
                    for j in range(JD):
                        for i in range(DH):
                            if j + 1 < JD:
                                decay(IT + j + 1, i)
                            if i == 1 and j > 0:
                                tanh_down(j - 1)
                    tanh_down(JD - 1)
                    for i in range(DH):
                        k = blk(b, h, i)
                        act.wait_ge(s_in, b * (2 * DB) + (DB + h * DH + i + 3))
                        if i >= 2:
                            act.wait_ge(s_y, k)
                        act.activation(tmp[:, 2 * (i % 2), :], psA[:, 1, :], ACT.Tanh, scale=0.5).then_inc(s_thz, 1)

        @block.tensor
        def _(pe):
            give_credits(pe, "tensor")
            at_gu = dtx[0:R, 0, :].rearrange("p (g h) -> p g h", g=2)
            b_gu = yT[0:R, :, :].rearrange("p a l -> p (a l)")[:, 0:2 * IT * IM].rearrange(
                "p (t g i) -> p t g i", g=2, i=IM)
            at_dn = xc[0:R, 0:2, :].rearrange("p a l -> p (a l)")[:, 0:IT * IM].rearrange("p (t i) -> p t i", i=IM)
            b_dn = dtx[0:R, 1, 0:H]
            pe.wait_ge(s_const, 16 * NCONST)
            with pe.Fori(0, IT // 2) as g:
                for t in range(2):
                    it = 2 * g + t
                    pe.wait_ge(s_af, it + 1)
                    for gu in range(2):
                        for k in range(HK):
                            mm = pe.matmul(psA[:, t, gu * 512 + k * IM:gu * 512 + (k + 1) * IM],
                                           at_gu[:, gu, k * P:(k + 1) * P], b_gu[:, it, gu, :], start=True, stop=True)
                    mm.then_inc(s_lr, 1)
            for it in range(IT):
                pe.wait_ge(s_af, IT + it + 1)
                pe.matmul(psA[0:IM, it % 2, 0:H], at_dn[:, it, :], b_dn, start=True, stop=True).then_inc(s_lr, 1)

            pe.wait_ge(s_ident, 2)
            after_wait(pe)
            with pe.Fori(0, NB) as b:
                for tb in range(TB):
                    pe.wait_ge(s_xn, b * TB + tb + 1)
                    pe.wait_ge(s_tact, t_use(b, tb) + 1)
                    for k in range(HK):
                        mm = pe.transpose(psT[:, tb % 2, k * P:(k + 1) * P], yT[:, tb, k * P:(k + 1) * P], ident[:, :])
                    mm.then_inc(s_tfa, 1)
                pe.wait_ge(s_tact, t_use(b, TB) + 2)
                after_wait(pe)

                def in_proj(t, dst):
                    for c in range(2):
                        for k in range(HK):
                            mm = pe.matmul(psA[:, dst, c * 512:(c + 1) * 512], w_is[:, t, k, :],
                                           xnT[:, k, c * 512:(c + 1) * 512], start=(k == 0), stop=(k == HK - 1))
                    return mm

                with pe.Fori(0, DB // 2) as g:
                    for t in range(2):
                        pe.wait_ge(s_wi[t], b * (16 * DB) + g * 16 + 16)
                        pe.wait_ge(s_af, a_use(b, 2 * g + t) + 1)
                        in_proj(t, t).then_inc(s_in, 1)
                pe.wait_ge(s_xc, b * DB + DB + 2)
                pe.wait_ge(s_wx, 16 * b + 16)
                pe.wait_ge(s_mf, b * M_USES + 2)
                for t in range(2):
                    for a in range(TB // 2):
                        tb = t * TB // 2 + a
                        for k in range(DB):
                            mm = pe.matmul(psM[:, t, a * E:(a + 1) * E], xc[:, k, tb * P:(tb + 1) * P], wx[:, k, :],
                                           start=(k == 0), stop=(k == DB - 1))
                    mm.then_inc(s_xp, 1)
                pe.wait_ge(s_sn, b + 1)
                for t in range(2):
                    pe.wait_ge(s_tact, t_use(b, TB + t) + 1)
                    after_wait(pe)
                    for a in range(TB // 2):
                        mm = pe.transpose(psT[0:E, t, a * P:(a + 1) * P], ssm[:, t * TB // 2 + a, :], ident[:, :])
                    mm.then_inc(s_tfa, 1)
                pe.wait_ge(s_tact, t_use(b, TB + 2) + 2)

                for h in range(HALVES):
                    pe.wait_ge(s_wdt, b * 48 + 16 + 32 * h)
                    for i in range(DH):
                        if i < 2:
                            pe.wait_ge(s_af, a_half(b, h, 0) + 2)
                        else:
                            pe.wait_ge(s_dtr, blk(b, h, i - 1))
                        m = (h * DH + i) * P
                        for c in range(2):
                            mm = pe.matmul(psA[:, i % 2, c * 512:(c + 1) * 512], wdt[:, m:m + P],
                                           ssT[0:R, c * 512:(c + 1) * 512], start=True, stop=True)
                        mm.then_inc(s_dtp, 1)

                    def turn(n, t, tb):
                        if tb == 0:
                            pe.wait_ge(s_scan, unit(b, h, n, DH) + 2)
                        pe.wait_ge(s_tdve, t_group(b, h, n, tb) + 1)
                        for i in range(DH):
                            mm = pe.transpose(psT[:, tb % 2, i * P:(i + 1) * P],
                                              hb[:, t * DH + i, tb * P:(tb + 1) * P], ident[:, :])
                        mm.then_inc(s_tfd, 1)

                    def gate_up(n, pair, t, q):
                        gu = q // 2
                        if q == 0:
                            pe.wait_ge(s_wt[t], b * (8 * HALVES * IT) + (8 * h * IT + 16) + pair * 16)
                        if q % 2 == 0:
                            pe.wait_ge(s_mf, m_half(b, h, 2 * n + gu) + 1)
                        for k in range(2 * (q % 2), 2 * (q % 2) + 2):
                            at = (gu * HK + k) * IM
                            mm = pe.matmul(psM[0:IM, gu, :], w_ts[:, t, at:at + IM],
                                           xnT[:, k, h * CH:(h + 1) * CH], start=(k == 0), stop=(k == HK - 1))
                        if q % 2 == 1:
                            mm.then_inc(s_fg if gu == 0 else s_fu, 1)

                    def down(j, q):
                        if q == 0:
                            pe.wait_ge(s_mf, m_half(b, h, 2 * IT + j) + 1)
                        if q == 3 and j == 0:
                            pe.wait_ge(s_mf, m_half(b, h, 2 * IT - 1) + 3)
                        for k in range(3 * q, 3 * q + 3):
                            mm = pe.matmul(psM[:, j % 2, :], hid[0:IM, k, j * P:(j + 1) * P], w_dn[0:IM, k, :],
                                           start=(k == 0), stop=(k == IT - 1))
                        if q == 3:
                            mm.then_inc(s_fd, 1)

                    with pe.Fori(0, IT // 2) as g:
                        for t in range(2):
                            for q in range(4):
                                turn(2 * g + t, t, 2 * q)
                                turn(2 * g + t, t, 2 * q + 1)
                                gate_up(2 * g + t, g, t, q)
                    for j in range(JD):
                        for q in range(4):
                            turn(IT + j, j % 2, 2 * q)
                            turn(IT + j, j % 2, 2 * q + 1)
                            down(j, q)
                    for i in range(DH):
                        pe.wait_ge(s_tdve, t_group(b, h, NS, 0) + 2)
                        pe.wait_ge(s_af, a_half(b, h, 2 * i) + 1)
                        for tb in range(TB):
                            mm = pe.transpose(psA[:, 0, tb * P:(tb + 1) * P], yT[:, tb, i * P:(i + 1) * P], ident[:, :])
                        mm.then_inc(s_yb, 1)
                        pe.wait_ge(s_wi[i % 2], b * (16 * DB) + 16 * (DB // 2 + h * DH // 2 + i // 2 + 1))
                        pe.wait_ge(s_af, a_half(b, h, 2 * i + 1) + 1)
                        in_proj(i % 2, 1).then_inc(s_in, 1)
                pe.wait_ge(s_wo, 16 * b + 16)
                pe.wait_ge(s_y, DB * b + DB + 1)
                for tb in range(TB):
                    pe.wait_ge(s_mf, m_half(b, HALVES, 0) + tb + 1)
                    for k in range(DB):
                        mm = pe.matmul(psM[:, tb % 2, :], xc[:, k, tb * P:(tb + 1) * P], hid[:, k, :],
                                       start=(k == 0), stop=(k == DB - 1))
                    mm.then_inc(s_sp, 1)

        @block.vector
        def _(dve):
            give_credits(dve, "vector")
            def stt(out, in0, scalar, in1, op0, op1):
                return dve.scalar_tensor_tensor(out=out, in0=in0, scalar=scalar, in1=in1, op0=op0, op1=op1)

            scale_gu = dt[:, 0:3, :].rearrange("p a l -> p (a l)")[:, 0:2 * IT * IM].rearrange(
                "p (t g i) -> p t g i", g=2, i=IM)
            scale_dn = dt[:, 3, 0:H]
            dve.wait_ge(s_const, 16 * NCONST)
            dve.tensor_scalar(hc, hc, 0.5, None, ALU.mult).then_inc(s_prep, 1)
            dve.wait_ge(s_negA, 1)
            dve.tensor_scalar(negA, negA, -1.0, None, ALU.mult).then_inc(s_prep, 1)
            flat = dt[:, :, :].rearrange("p a l -> p (a l)")
            dve.tensor_scalar(flat[:, 0:2 * IT * IM], flat[:, 0:2 * IT * IM], Q_STEP, None, ALU.mult).then_inc(s_prep, 1)
            dve.tensor_scalar(scale_dn, scale_dn, Q_STEP, None, ALU.mult).then_inc(s_prep, 1)
            dve.wait_ge(s_prep, 4)
            with dve.Fori(0, IT // 2) as g:
                for t in range(2):
                    it = 2 * g + t
                    dve.wait_ge(s_q[t], g * 16 + 16)
                    dve.wait_ge(s_wst[t], g * 16 + 16)
                    for gu in range(2):
                        sl = slice(gu * HK * IM, (gu + 1) * HK * IM)
                        ins = stt(tmp[:, t, sl].rearrange("p (k i) -> p k i", k=HK),
                                  qs[:, t, sl].rearrange("p (k i) -> p k i", k=HK), -Q_ZERO,
                                  scale_gu[:, bass.ds(it, 1), gu, :].to_broadcast([P, HK, IM]), ALU.add, ALU.mult)
                    ins.then_inc(s_deq, 1)
                    dve.wait_ge(s_deq, it + 3)
                    dve.wait_ge(s_lr, it + 1)
                    w = tmp[:, t, 0:2 * HK * IM].rearrange("p (g c) -> p g c", g=2)
                    ps = psA[:, t, :].rearrange("p (g c) -> p g c", g=2)[:, :, 0:HK * IM]
                    stt(w, ps, LR_SCALE, w, ALU.mult, ALU.add).then_inc(s_af, 1)
            for t in range(2):
                dve.wait_ge(s_wst[t], 16 + 16 * IT // 2)
            after_wait(dve)
            with dve.Fori(0, IT // 2) as g:
                for t in range(2):
                    it = 2 * g + t
                    dve.wait_ge(s_q[t], g * 16 + 16 * (IT // 2 + 1))
                    dve.wait_ge(s_af, it + IT)
                    stt(tmp[0:IM, t, 0:H], qs[0:IM, t, 0:H], -Q_ZERO, scale_dn[0:IM, :], ALU.add, ALU.mult
                        ).then_inc(s_deq, 1)
                    dve.wait_ge(s_deq, it + IT + 3)
                    dve.wait_ge(s_lr, it + IT + 1)
                    stt(w_dn[0:IM, it, :], psA[0:IM, t, 0:H], LR_SCALE, tmp[0:IM, t, 0:H], ALU.mult, ALU.add
                        ).then_inc(s_af, 1)

            with dve.Fori(0, NB) as b:
                dve.wait_ge(s_x, 16 * b + 16)
                for tb in range(TB):
                    dve.bn_stats(st[:, tb, :], yT[:, tb, :]).then_inc(s_st, 1)
                for tb in range(TB):
                    dve.wait_ge(s_st, b * TB + tb + 1)
                    after_wait(dve)
                    dve.bn_aggr(mv[:, tb, :], st[:, tb, :]).then_inc(s_mv, 1)
                dve.wait_ge(s_std, b + 1)
                dve.reciprocal(rs[:, :], rs[:, :]).then_inc(s_rstd, 1)
                dve.wait_ge(s_rstd, b + 1)
                stt(nm[:, :], mv[:, :, 0], -1.0, rs[:, :], ALU.mult, ALU.mult).then_inc(s_nm, 1)
                with dve.Fori(0, DB // 2) as g:
                    for t in range(2):
                        m = 2 * g + t
                        dve.wait_ge(s_acc, b * DB + m + 1)
                        for k in range(KC - 2, -1, -1):
                            lag = KC - 1 - k
                            if k < KC - 2:
                                dve.wait_ge(s_tap, b * (2 * DB) + 2 * m + lag - 1)
                            ins = stt(tmp[:, t, lag:L], psA[:, t, 0:L - lag], hc[:, m, k:k + 1], tmp[:, t, lag:L],
                                      ALU.mult, ALU.add)
                            ins.then_inc(s_tap if k else s_af, 1)
                        dve.wait_ge(s_thc, b * DB + m + 1)
                        stt(xc[:, m, :], tmp[:, 2 + t, :], 1.0, tmp[:, t, :], ALU.add, ALU.mult).then_inc(s_xc, 1)
                dve.wait_ge(s_sq, 2 * b + 2)
                dve.tensor_reduce(ms[:, :, 0:1], sq[:, :, 0:R], AX.X, ALU.add).then_inc(s_ms, 1)
                dve.tensor_reduce(ms[:, :, 1:3], sq[:, :, R:E].rearrange("p a (g n) -> p a g n", g=2), AX.X,
                                  ALU.add).then_inc(s_ms, 1)
                dve.wait_ge(s_rms, 2 * b + 2)
                dve.reciprocal(ms[:, :, :], ms[:, :, :]).then_inc(s_rinv, 1)
                dve.wait_ge(s_rinv, b + 1)
                dve.wait_ge(s_xpr, 2 * b + 2)
                for g, (lo, hi) in enumerate([(0, R), (R, R + NS), (R + NS, E)]):
                    dve.tensor_tensor(ssm[:, :, lo:hi], ssm[:, :, lo:hi],
                                      ms[:, :, g:g + 1].to_broadcast([P, TB, hi - lo]), ALU.mult).then_inc(s_sn1, 1)
                dve.wait_ge(s_sn1, 3 * b + 3)
                dve.tensor_tensor(ssm[:, :, :], ssm[:, :, :],
                                  lnw[:, :].rearrange("p (a e) -> p a e", a=1).to_broadcast([P, TB, E]), ALU.mult
                                  ).then_inc(s_sn, 1)

                for h in range(HALVES):
                    for i in range(DH):
                        k = blk(b, h, i)
                        t = 2 * (i % 2)
                        dve.wait_ge(s_w1, k + 1)
                        stt(tmp[:, t, :], tmp[:, t + 1, :], -1.0, tmp[:, t, :], ALU.add, ALU.subtract).then_inc(s_nd, 1)
                        dve.wait_ge(s_nd, k + 1)
                        dve.wait_ge(s_rl, k + 1)
                        dve.tensor_tensor(dt[:, i, :], dt[:, i, :], tmp[:, t, :], ALU.subtract).then_inc(s_dt, 1)

                    def scan(n, t, i):
                        dve.wait_ge(s_a, unit(b, h, n, i) + 1)
                        dve.wait_ge(s_u, unit(b, h, n, i) + 9)
                        dve.tensor_tensor_scan(hb[:, t * DH + i, :], psA[:, i % 2, :], ub[:, i % 2, :], 0.0,
                                               ALU.mult, ALU.add).then_inc(s_scan, 1)

                    def add_y(n, tb):
                        dve.wait_ge(s_tfd, t_group(b, h, n, tb) + 1)
                        if h or n is not FIRST:
                            dve.wait_ge(s_tdve, t_group(b, h, n - 1, tb) + 3)
                        stt(yT[:, tb, :], psT[:, tb % 2, :], ssm[:, tb, bass.ds(n + (R + NS), 1)], yT[:, tb, :],
                            ALU.mult, ALU.add).then_inc(s_tdve, 1)

                    def silu_gate(n, t):
                        dve.wait_ge(s_th, b * (HALVES * NS) + h * NS + n + 1)
                        stt(th[0:IM, t, :], th[0:IM, t, :], 1.0, psM[0:IM, 0, :], ALU.add, ALU.mult).then_inc(s_mf, 1)

                    def hidden(n, t):
                        dve.wait_ge(s_fu, ffn(b, h, n) + 3)
                        dve.wait_ge(s_mf, m_half(b, h, 2 * n) + 3)
                        stt(hid[0:IM, n, :], th[0:IM, t, :], 0.5, psM[0:IM, 1, :], ALU.mult, ALU.mult).then_inc(s_mf, 1)

                    def silu_down(j):
                        dve.wait_ge(s_th, b * (HALVES * NS) + (h * NS + IT + j + 1))
                        stt(th[:, j % 2, :], th[:, j % 2, :], 1.0, psM[:, j % 2, :], ALU.add, ALU.mult).then_inc(s_mf, 1)

                    def slot(n, t, last=False, gate=None, up=None, dn=None):
                        for i in range(DH):
                            if not last:
                                scan(n + 1, 1 - t, i)
                            add_y(n, 2 * i)
                            if i == DH - 1 and gate is not None:
                                silu_gate(gate, t)
                            add_y(n, 2 * i + 1)
                            if i == 0 and up is not None:
                                hidden(up, 1 - t)
                            if i == 1 and dn is not None:
                                silu_down(dn)

                    dve.wait_ge(s_yz, b * HALVES + h + 1)
                    for i in range(DH):
                        scan(0, 0, i)
                    slot(FIRST, 0, gate=0)
                    with dve.Fori(0, IT // 2 - 1) as g:
                        slot(2 * g + 1, 1, gate=2 * g + 1, up=2 * g)
                        slot(2 * g + 2, 0, gate=2 * g + 2, up=2 * g + 1)
                    slot(IT - 1, 1, gate=IT - 1, up=IT - 2)
                    slot(IT, 0, up=IT - 1)
                    for j in range(1, JD):
                        slot(IT + j, j % 2, last=(j == JD - 1), dn=j - 1)
                    silu_down(JD - 1)
                    for i in range(DH):
                        k, m, t = blk(b, h, i), h * DH + i, 2 * (i % 2)
                        dve.wait_ge(s_yb, k + 1)
                        stt(xc[:, m, :], xc[:, m, :], cc[:, m, DP:DP + 1], psA[:, 0, :], ALU.mult, ALU.add).then_inc(s_af, 1)
                        dve.wait_ge(s_thz, k + 1)
                        stt(tmp[:, t + 1, :], tmp[:, t, :], 1.0, psA[:, 1, :], ALU.add, ALU.mult).then_inc(s_af, 1)
                        dve.wait_ge(s_af, a_half(b, h, 2 * i + 1) + 3)
                        stt(xc[:, m, :], xc[:, m, :], 0.5, tmp[:, t + 1, :], ALU.mult, ALU.mult).then_inc(s_y, 1)
                dve.wait_ge(s_xg, 32 * b + 32)
                for tb in range(TB):
                    dve.wait_ge(s_sp, b * TB + tb + 1)
                    stt(gt[:, tb, :], psM[:, tb % 2, :], 0.5, gt[:, tb, :], ALU.mult, ALU.mult).then_inc(s_mf, 1)


def kernel(**inputs):
    import concourse.bacc as bacc
    from concourse.bass_utils import run_bass_kernel_spmd

    def arr(name):
        return np.asarray(inputs[name])

    def pad(a, axis):
        width = [(0, 0)] * a.ndim
        width[axis] = (0, IT * IM - I)
        return np.pad(a, width)

    def per_channel(a):
        return a.reshape(DB, P, -1).transpose(1, 0, 2)

    def ffn_in(q):
        return pad(q, 0).reshape(IT, IM, HK, P).transpose(0, 3, 2, 1)

    A, F = "L0_attn_", "L0_ffn_"
    gu = ("gate", "up")
    data = {
        "x": arr(A + "hidden_states"),
        "w_in": arr(A + "in_proj_w").reshape(HK, P, 2 * DB, P).transpose(2, 1, 0, 3),
        "chan": np.concatenate([per_channel(arr(A + n)) for n in ("conv_w", "conv_b", "dt_bias", "D_param", "A_log")], 2),
        "w_x": per_channel(arr(A + "x_proj_w").T),
        "w_dt": arr(A + "dt_proj_w").T,
        "ln_w": np.concatenate([arr(A + n) for n in ("dt_ln_w", "B_ln_w", "C_ln_w")])[None],
        "w_out": per_channel(arr(A + "out_proj_w").T),
        "gu_q": np.stack([ffn_in(arr(F + n + "_q")) for n in gu], 2).reshape(IT, P, 2 * HK * IM),
        "gu_s": np.stack([pad(arr(F + n + "_scale"), 0).reshape(IT, IM) for n in gu], 1).reshape(1, -1),
        "gu_at": np.stack([arr(F + n + "_A").T for n in gu], 1),
        "gu_b": np.stack([pad(arr(F + n + "_B"), 1).reshape(R, IT, IM) for n in gu], 2).reshape(R, -1),
        "dn_q": pad(arr(F + "down_q").T, 0).reshape(IT, IM, H),
        "dn_s": arr(F + "down_scale")[None],
        "dn_at": pad(arr(F + "down_A"), 0).T,
        "dn_b": arr(F + "down_B"),
    }
    data = {f"{n}_dram": np.ascontiguousarray(a) for n, a in data.items()}
    nc = bacc.Bacc("TRN2", target_bir_lowering=False, num_devices=1)
    args = [nc.dram_tensor(n, a.shape, mybir.dt.from_np(a.dtype), kind="ExternalInput").ap() for n, a in data.items()]
    args.append(nc.dram_tensor("out_dram", (NB, L, H), F32, kind="ExternalOutput").ap())
    build(nc, *args)
    r = run_bass_kernel_spmd(nc, [data], core_ids=[0])
    return r.results[0]["out_dram"]
```

```python
from contextlib import ExitStack

import numpy as np

import concourse.bass as bass
from concourse import mybir

F32 = mybir.dt.float32
I32 = mybir.dt.int32
ALU = mybir.AluOpType
ACT = mybir.ActivationFunctionType
AX = mybir.AxisListType

P = 128
NB, L, H = 2, 1024, 512
D, NS, R, KC = 1024, 16, 32, 4
E = R + 2 * NS
I = 1376
IT = 12
IM = 116
HK, DB, TB = H // P, D // P, L // P
HALVES, DH = 2, DB // 2
CH = L // HALVES
JD = CH // P
LN_EPS, RMS_EPS = 1e-5, 1e-6
Q_ZERO, Q_STEP, LR_SCALE = 7.5, 0.005, 0.02
CW, CB, DTB, DP, AL = 0, KC, KC + 1, KC + 2, KC + 3
NCC = AL + NS

FILL = 4
MIX = [("z", 0), ("z", 1), ("g", 0), ("z", 2), ("g", 1), ("z", 3), ("g", 2), ("g", 3)]
W_USES = 2 * DB + HALVES * IT
FILL_AT = [[[], [0], [1], [2]], [[], [0], [1], [2]]]


def w_z(h, i):
    return DB + IT + MIX.index(("z", i)) if h == 0 else W_USES - DH + i


def w_g(h, n):
    if h == 0:
        return DB + n
    return DB + IT + (MIX.index(("g", n)) if n < FILL else DH + n)


T_ACT = TB + 2
T_DVE = HALVES * NS * TB
LR_USES = 3 * IT
PT = 3
A_USES = 2 * DB
M_HALF = 2 * IT + JD
M_USES = HALVES * M_HALF + TB
DOWN = IT - FILL

def build(nc, x, w_in, chan, w_x, w_dt, ln_w, w_out, gu_q, gu_s, gu_at, gu_b, dn_q, dn_s, dn_at, dn_b, out):
    ctx = ExitStack()
    with ctx:
        def sb(name, shape, dt=F32):
            return ctx.enter_context(nc.sbuf_tensor(name, shape, dt))

        def sem(name):
            return ctx.enter_context(nc.semaphore(name))

        w_gu = nc.dram_tensor("w_gu_scratch", [IT, P, 2 * HK * IM], F32).ap()
        ss_rows = nc.dram_tensor("ss_rows_scratch", [NB, E, L], F32).ap()
        g_rows = nc.dram_tensor("g_scratch", [NB, L, H], F32).ap()

        xnT = sb("xnT", [P, HK, L])
        xc = sb("xc", [P, DB, L])
        dt = sb("dt", [P, DH, L])
        dtx = sb("dtx", [P, DH, L])
        yT = sb("yT", [P, TB, DH * P])
        hb = sb("hb", [P, 2 * DH, L])
        ub = sb("ub", [P, 2, L])
        bn = sb("bn", [P, 2, L])
        hid = sb("hid", [P, IT, CH])
        w_dn = sb("w_dn", [P, IT, H])
        w_ts = sb("w_ts", [P, 2, 2 * HK * IM])
        th = sb("th", [P, 2, CH])
        ident = sb("ident", [P, P])
        cc = sb("cc", [P, DB, NCC])
        lnw = sb("lnw", [P, E])
        st = sb("st", [P, TB, 6])
        mv = sb("mv", [P, TB, 2])
        rs = sb("rs", [P, TB])
        nm = sb("nm", [P, TB])
        ssm = sb("ssm", [P, TB, E])
        ms = sb("ms", [P, TB, 3])
        tmp = hb
        wx = hb[:, DH, 0:DB * E].rearrange("p (k e) -> p k e", e=E)
        ssT = hb[0:E, DH + 1, :]
        wdt = hb[0:R, DH + 2, 0:D]
        sq = hb[:, DH + 3, 0:TB * E].rearrange("p (a e) -> p a e", e=E)
        xt = dt[:, :, :].rearrange("p i (s c) -> p (i s) c", c=H)
        gt = dtx[:, :, :].rearrange("p i (s c) -> p (i s) c", c=H)
        hid_flat = hid[:, :, :].rearrange("p a c -> p (a c)")
        dt_flat = dt[:, :, :].rearrange("p a c -> p (a c)")
        dtx_flat = dtx[:, :, :].rearrange("p a c -> p (a c)")
        WT = 2 * HK * IM
        qs = hid_flat[:, 0:2 * WT].rearrange("p (t c) -> p t c", t=2).bitcast(I32)
        wf = hid_flat[:, 2 * WT:4 * WT].rearrange("p (t c) -> p t c", t=2)
        at_gu = hid_flat[0:R, 4 * WT:4 * WT + 2 * H]
        at_dn = hid_flat[0:R, 4 * WT + 2 * H:4 * WT + 2 * H + IT * IM]
        b_gu = dtx_flat[0:R, 0:2 * IT * IM]
        b_dn = dtx_flat[0:R, 2 * IT * IM:2 * IT * IM + H]
        scales = dt_flat[:, 0:2 * IT * IM + H]
        w_is = w_ts[:, :, 0:HK * P].rearrange("p t (k j) -> p t k j", k=HK)
        hc = cc[:, :, CW:CB + 1]
        negA = cc[:, :, AL:AL + NS]

        psA = ctx.enter_context(nc.psum_tensor("psA", [P, 2, L], F32))
        psT = ctx.enter_context(nc.psum_tensor("psT", [P, 2, 512], F32))
        psM = ctx.enter_context(nc.psum_tensor("psM", [P, 2, 512], F32))

        s_past = sem("s_past")
        s_const = sem("s_const")
        s_fc = sem("s_fc")
        s_ident = sem("s_ident")
        s_negA = sem("s_negA")
        s_prep = sem("s_prep")
        s_q = [sem("s_q0"), sem("s_q1")]
        s_scl = sem("s_scl")
        s_lr = sem("s_lr")
        s_deq = sem("s_deq")
        s_lrr = sem("s_lrr")
        s_wst = [sem("s_wst0"), sem("s_wst1")]
        s_x = sem("s_x")
        s_st = sem("s_st")
        s_mv = sem("s_mv")
        s_std = sem("s_std")
        s_rstd = sem("s_rstd")
        s_nm = sem("s_nm")
        s_xn = sem("s_xn")
        s_tact = sem("s_T_act")
        s_tdve = sem("s_T_dve")
        s_tfa = sem("s_Ta_full")
        s_tfd = sem("s_Td_full")
        s_af = sem("s_A_free")
        s_mf = sem("s_M_free")
        s_w = [sem("s_w0"), sem("s_w1")]
        s_wp = sem("s_wp")
        s_acc = sem("s_acc")
        s_tap = sem("s_tap")
        s_thc = sem("s_thc")
        s_xc = sem("s_xc")
        s_wx = sem("s_wx")
        s_wdt = sem("s_wdt")
        s_xp = sem("s_xp")
        s_xpr = sem("s_xpr")
        s_sq = sem("s_sq")
        s_ms = sem("s_ms")
        s_rms = sem("s_rms")
        s_rinv = sem("s_rinv")
        s_sn1 = sem("s_sn1")
        s_sn = sem("s_sn")
        s_bst = sem("s_bst")
        s_dtp = sem("s_dtp")
        s_dtr = sem("s_dtr")
        s_abs = sem("s_abs")
        s_e = sem("s_e")
        s_e1 = sem("s_e1")
        s_ln = sem("s_ln")
        s_nd = sem("s_nd")
        s_rl = sem("s_rl")
        s_dt = sem("s_dt")
        s_dtx = sem("s_dtx")
        s_yz = sem("s_yz")
        s_B = [sem("s_B0"), sem("s_B1")]
        s_u = sem("s_u")
        s_a = sem("s_a")
        s_scan = sem("s_scan")
        s_fg = sem("s_fg")
        s_fd = sem("s_fd")
        s_th = sem("s_th")
        s_gst = [sem("s_gst0"), sem("s_gst1")]
        s_yb = sem("s_yb")
        s_ybr = sem("s_ybr")
        s_zv = sem("s_zv")
        s_thz = sem("s_thz")
        s_y = sem("s_y")
        s_wo = sem("s_wo")
        s_xg = sem("s_xg")
        s_sp = sem("s_sp")
        s_o = sem("s_o")
        s_out = sem("s_out")
        CREDITS = {
            "vector": [(s_tdve, 2), (s_af, 2), (s_mf, 2), (s_deq, 2), (s_lrr, 3), (s_xc, 2), (s_scan, 2), (s_y, 1), (s_ybr, 1)],
            "scalar": [(s_tact, 2), (s_wst[0], 16), (s_wst[1], 16)],
            "tensor": [(s_wp, 2)],
            "gpsimd": [(s_u, 8)],
            "sync": [(s_gst[0], 16), (s_gst[1], 16), (s_out, 16)],
        }

        def t_use(b, j):
            return b * T_ACT + j

        def t_group(b, h, n, tb):
            return b * T_DVE + h * (NS * TB) + n * TB + tb

        def a_use(b, j):
            return b * A_USES + j

        def w_use(b, off):
            return b * W_USES + off

        def landed(b, off):
            return b * (8 * W_USES) + 16 * (off // 2 + 1)

        def m_half(b, h, j):
            return b * M_USES + h * M_HALF + j

        def unit(b, h, n, i):
            return b * (HALVES * NS * DH) + h * NS * DH + n * DH + i

        def ffn(b, h, n):
            return b * (HALVES * IT) + h * IT + n

        def soft_tmp(i):
            return (2, 3) if i % 2 == 0 else (DH, DH + 3)

        def dt_buf(h, i):
            return i % 2 if h == 0 else 0

        def blk(b, h, i):
            return b * DB + h * DH + i

        def lr_bank(use):
            return psM[:, 1, :] if use % 3 == 0 else psT[:, use % 3 - 1, :]

        def b_loads(b, h, pair):
            return b * (16 * HALVES * NS // 2) + (16 * (h * NS // 2 + 1)) + pair * 16

        def give_credits(engine, name):
            for s, n in CREDITS[name]:
                engine.sem_inc(s, n)

        def after_wait(engine):
            engine.sem_inc(s_past, 1)

        block = ctx.enter_context(nc.Block())

        @block.sync
        def _(sp):
            give_credits(sp, "sync")
            def load_x(b):
                sp.dma_start(yT[:, :, :], x[b].rearrange("(a p) h -> p a h", p=P)).then_inc(s_x, 16)

            def load_small():
                sp.dma_start(wx, w_x).then_inc(s_wx, 16)
                sp.dma_start(wdt, w_dt).then_inc(s_wdt, 16)

            def load_w_in(b, m):
                sp.wait_ge(s_wp, w_use(b, m) + 1)
                sp.dma_start(w_is[:, m % 2, :, :], w_in[m]).then_inc(s_w[m % 2], 16)

            def load_q(it):
                t = it % 2
                sp.wait_ge(s_deq, it + 1)
                if it < IT:
                    sp.dma_start(qs[:, t, :], gu_q[it]).then_inc(s_q[t], 16)
                else:
                    sp.dma_start(qs[0:IM, t, 0:H], dn_q[it - IT]).then_inc(s_q[t], 16)

            load_x(0)
            sp.dma_start(cc[:, :, :], chan).then_inc(s_const, 16)
            sp.dma_start(lnw[:, :], ln_w.to_broadcast([P, E])).then_inc(s_const, 16)
            load_w_in(0, 0)
            sp.dma_start(scales[:, 0:2 * IT * IM], gu_s.to_broadcast([P, 2 * IT * IM])).then_inc(s_fc, 16)
            sp.dma_start(scales[:, 2 * IT * IM:], dn_s.to_broadcast([P, H])).then_inc(s_fc, 16)
            load_q(0)
            load_w_in(0, 1)
            load_q(1)
            sp.dma_start(at_gu, gu_at.rearrange("r g h -> r (g h)")).then_inc(s_fc, 16)
            sp.dma_start(b_gu, gu_b).then_inc(s_fc, 16)
            sp.dma_start(at_dn, dn_at).then_inc(s_fc, 16)
            sp.dma_start(b_dn, dn_b).then_inc(s_fc, 16)
            load_small()

            for b in range(NB):
                for m in range(DB):
                    if m + 2 < DB:
                        load_w_in(b, m + 2)
                    if b == 0:
                        for it in range(PT * m + 2, min(PT * m + PT + 2, 2 * IT)):
                            load_q(it)
                sp.wait_ge(s_tact, t_use(b, TB + 2) + 2)
                sp.dma_start(ss_rows[b], ssT).then_inc(s_bst, 16)
                sp.wait_ge(s_bst, 16 * b + 16)
                after_wait(sp)

                for h in range(HALVES):
                    def load_b(n, t):
                        sp.wait_ge(s_u, unit(b, h, n, 0) + 4)
                        sp.dma_start(bn[:, t, :], ss_rows[b, bass.ds(n + R, 1), :].to_broadcast([P, L])).then_inc(s_B[t], 16)

                    def load_g(n, off):
                        sp.wait_ge(s_wp, w_use(b, off) + 1)
                        sp.dma_start(w_ts[:, t, :], w_gu[n]).then_inc(s_w[t], 16)

                    def load_z(hz, i):
                        off = w_z(hz, i)
                        sp.wait_ge(s_wp, w_use(b, off) + 1)
                        sp.dma_start(w_is[:, off % 2, :, :], w_in[DB + hz * DH + i]).then_inc(s_w[off % 2], 16)

                    def store_gate(j):
                        sp.wait_ge(s_mf, m_half(b, h, 2 * IT + j) + 3)
                        sp.dma_start(g_rows[b, (h * JD + j) * P:(h * JD + j + 1) * P, :], th[:, j % 2, :]
                                     ).then_inc(s_gst[j % 2], 16)

                    if h == 0:
                        if b == 0:
                            for t in range(2):
                                sp.wait_ge(s_wst[t], 16 + 16 * IT // 2)
                            after_wait(sp)
                        for n in range(FILL):
                            t = w_g(h, n) % 2
                            load_g(n, w_g(h, n))
                    with sp.Fori(0, DOWN // 2) as g:
                        for t in range(2):
                            load_b(2 * g + t, t)
                            load_g(2 * g + (FILL + t), 2 * g + (w_g(h, FILL) + t))
                    for n in range(DOWN, NS):
                        load_b(n, n % 2)
                        if n < DOWN + 2:
                            load_z(h, n - DOWN)
                        if n >= DOWN + 4 and n % 2 == 0:
                            store_gate((n - DOWN) // 2 - 2)
                    store_gate(JD - 2)
                    store_gate(JD - 1)
                    if h == 0:
                        sp.wait_ge(s_tfd, t_group(b, h, NS, 0))
                        sp.dma_start(wdt, w_dt).then_inc(s_wdt, 16)
                        sp.dma_start(ssT[0:R, :], ss_rows[b, 0:R, :]).then_inc(s_wdt, 16)
                        for kind, i in MIX[2:]:
                            if kind == "z":
                                load_z(h, i)
                            else:
                                t = w_g(1, i) % 2
                                load_g(i, w_g(1, i))
                    else:
                        load_z(h, 2)
                        load_z(h, 3)

                sp.wait_ge(s_fd, b * TB + TB)
                sp.dma_start(hid[:, 0:DB, :], w_out).then_inc(s_wo, 16)
                sp.wait_ge(s_a, unit(b, HALVES, 0, 0))
                sp.dma_start(xt, x[b].rearrange("(a p) h -> p a h", p=P)).then_inc(s_xg, 16)
                sp.wait_ge(s_u, unit(b, HALVES, 0, 0) + 8)
                for t in range(2):
                    sp.wait_ge(s_gst[t], b * (16 * TB // 2) + (16 * TB // 2 + 16))
                sp.dma_start(gt, g_rows[b].rearrange("(a p) h -> p a h", p=P)).then_inc(s_xg, 16)
                if b + 1 < NB:
                    sp.wait_ge(s_tfd, t_group(b, HALVES, 0, 0))
                    load_small()
                    sp.wait_ge(s_yb, blk(b, HALVES, 0))
                    load_x(b + 1)
                    load_w_in(b + 1, 0)
                    load_w_in(b + 1, 1)
                with sp.Fori(0, TB) as tb:
                    sp.wait_ge(s_o, b * TB + tb + 1)
                    sp.dma_start(out[b, bass.ts(tb, P), :], xt[:, tb, :]).then_inc(s_out, 16)
            sp.wait_ge(s_out, NB * TB * 16 + 16)

        @block.gpsimd
        def _(pool):
            give_credits(pool, "gpsimd")
            pool.memset(ident[:, :], 0.0).then_inc(s_ident, 1)
            pool.wait_ge(s_ident, 1)
            pool.affine_select(out=ident[:, :], in_=ident[:, :], compare_op=ALU.not_equal, fill=1.0,
                               base=0, pattern=[[-1, P]], channel_multiplier=1).then_inc(s_ident, 1)
            def layer_norm(b):
                pool.wait_ge(s_nm, b + 1)
                after_wait(pool)
                for tb in range(TB):
                    pool.tensor_scalar(yT[:, tb, :], yT[:, tb, :], rs[:, tb:tb + 1], nm[:, tb:tb + 1],
                                       ALU.mult, ALU.add).then_inc(s_xn, 1)

            layer_norm(0)
            for b in range(NB):
                for h in range(HALVES):
                    for i in range(DH):
                        k = blk(b, h, i)
                        pool.wait_ge(s_dt, k + 1)
                        pool.tensor_tensor(dtx[:, i, :], dt[:, i, :], xc[:, h * DH + i, :],
                                           ALU.mult).then_inc(s_dtx, 1)
                        if (h == 0 and i == 0) or (h > 0 and i == DH - 1):
                            pool.wait_ge(s_tfa, t_use(b, TB))
                            if h:
                                pool.wait_ge(s_yb, blk(b, h, 0))
                            after_wait(pool)
                            pool.memset(yT[:, :, :], 0.0).then_inc(s_yz, 1)
                    pool.wait_ge(s_dtx, blk(b, h, DH))
                    after_wait(pool)

                    def inputs(n, pair, t):
                        pool.wait_ge(s_B[t], b_loads(b, h, pair))
                        for i in range(DH):
                            pool.wait_ge(s_scan, unit(b, h, n, i) + 1)
                            pool.tensor_tensor(ub[:, i % 2, :], dtx[:, i, :], bn[:, t, :], ALU.mult).then_inc(s_u, 1)

                    with pool.Fori(0, NS // 2) as g:
                        for t in range(2):
                            inputs(2 * g + t, g, t)
                pool.wait_ge(s_xg, 32 * b + 32)
                after_wait(pool)
                def add_x(tb):
                    pool.wait_ge(s_mf, m_half(b, HALVES, 0) + tb + 3)
                    pool.tensor_tensor(xt[:, tb, :], xt[:, tb, :], gt[:, tb, :], ALU.add).then_inc(s_o, 1)

                add_x(0)
                if b + 1 < NB:
                    layer_norm(b + 1)
                for tb in range(1, TB):
                    add_x(tb)

        @block.scalar
        def _(act):
            give_credits(act, "scalar")
            def layer_norm(b):
                act.wait_ge(s_mv, b * TB + TB)
                act.activation(rs[:, :], mv[:, :, 1], ACT.Sqrt, bias=LN_EPS).then_inc(s_std, 1)
                for tb in range(TB):
                    act.wait_ge(s_tfa, t_use(b, tb) + 1)
                    act.activation(xnT[:, :, tb * P:(tb + 1) * P],
                                   psT[:, tb % 2, :].rearrange("p (k t) -> p k t", k=HK),
                                   ACT.Copy).then_inc(s_tact, 1)

            act.wait_ge(s_const, 32)
            act.activation(negA, negA, ACT.Exp).then_inc(s_negA, 1)
            layer_norm(0)
            for b in range(NB):
                def start_conv(m):
                    act.wait_ge(s_wp, w_use(b, m) + 3)
                    act.wait_ge(s_xc, b * DB + m + 1)
                    act.activation(tmp[:, m % 2, :], psA[:, m % 2, :], ACT.Identity,
                                   bias=hc[:, m, KC:KC + 1], scale=hc[:, m, KC - 1:KC]).then_inc(s_acc, 1)

                act.wait_ge(s_prep, 2)
                act.wait_ge(s_y, b * DB + 1)
                start_conv(0)
                for m in range(DB):
                    if m + 1 < DB:
                        start_conv(m + 1)
                    act.wait_ge(s_af, a_use(b, m) + 3)
                    act.activation(tmp[:, 2 + m % 2, :], tmp[:, m % 2, :], ACT.Tanh).then_inc(s_thc, 1)
                    if b == 0:
                        for it in range(PT * m, min(PT * (m + 1), IT)):
                            act.wait_ge(s_lrr, 2 * it + 5)
                            act.dma_start(w_gu[it], wf[:, it % 2, :]).then_inc(s_wst[it % 2], 16)
                v = psM[:, 0, :].rearrange("p (a e) -> p a e", e=E)
                act.wait_ge(s_xp, b + 1)
                act.activation(sq, v, ACT.Square).then_inc(s_sq, 1)
                act.activation(ssm[:, :, :], v, ACT.Copy).then_inc(s_xpr, 1)
                act.wait_ge(s_ms, 2 * b + 2)
                act.activation(ms[:, :, 0:1], ms[:, :, 0:1], ACT.Sqrt, bias=RMS_EPS, scale=1.0 / R).then_inc(s_rms, 1)
                act.activation(ms[:, :, 1:3], ms[:, :, 1:3], ACT.Sqrt, bias=RMS_EPS, scale=1.0 / NS).then_inc(s_rms, 1)
                for t in range(2):
                    act.wait_ge(s_tfa, t_use(b, TB + t) + 1)
                    act.activation(ssT[:, t * 512:(t + 1) * 512], psT[0:E, t, :], ACT.Copy).then_inc(s_tact, 1)

                for h in range(HALVES + 1):
                    def softplus(i):
                        k = blk(b, h, i)
                        e, w = soft_tmp(i)
                        bias = cc[:, h * DH + i, DTB:DTB + 1]
                        act.wait_ge(s_dtp, k + 1)
                        if i >= 2:
                            act.wait_ge(s_dt, k - 1)
                        act.activation(tmp[:, e, :], psA[:, dt_buf(h, i), :], ACT.Abs, bias=bias).then_inc(s_abs, 1)
                        act.activation(dt[:, i, :], psA[:, dt_buf(h, i), :], ACT.Relu, bias=bias).then_inc(s_dtr, 1)
                        act.wait_ge(s_abs, k + 1)
                        act.activation(tmp[:, e, :], tmp[:, e, :], ACT.Exp, scale=-1.0).then_inc(s_e, 1)
                        act.wait_ge(s_e, k + 1)
                        act.activation(tmp[:, w, :], tmp[:, e, :], ACT.Identity, bias=1.0).then_inc(s_e1, 1)
                        act.wait_ge(s_e1, k + 1)
                        act.wait_ge(s_nd, k + 1)
                        act.activation(tmp[:, w, :], tmp[:, w, :], ACT.Ln).then_inc(s_ln, 1)

                    def tanh_z(i):
                        act.wait_ge(s_wp, w_use(b, w_z(h - 1, i)) + 3)
                        if i >= 2:
                            act.wait_ge(s_y, blk(b, h - 1, i))
                        act.activation(tmp[:, i % 2, :], psA[:, 1, :], ACT.Tanh, scale=0.5).then_inc(s_thz, 1)

                    def decay(n, i):
                        act.wait_ge(s_scan, unit(b, h, n, i) + 1)
                        act.activation(psA[:, i % 2, :], dt[:, i, :], ACT.Exp,
                                       scale=negA[:, h * DH + i, bass.ds(n, 1)]).then_inc(s_a, 1)

                    def tanh_gate(n, t):
                        act.wait_ge(s_fg, ffn(b, h, n) + 1)
                        act.activation(th[0:IM, t, :], psM[0:IM, 0, :], ACT.Tanh, scale=0.5).then_inc(s_th, 1)

                    def tanh_down(j):
                        act.wait_ge(s_fd, b * TB + h * JD + j + 1)
                        if j < 2:
                            act.wait_ge(s_mf, m_half(b, h, 2 * (IT - 2 + j) + 1) + 3)
                        else:
                            act.wait_ge(s_gst[j % 2], b * (16 * TB // 2) + 16 * (h * JD // 2 + j // 2 + 1))
                        act.activation(th[:, j % 2, :], psM[:, j % 2, :], ACT.Tanh, scale=0.5).then_inc(s_th, 1)

                    if h == HALVES:
                        for i in range(DH):
                            tanh_z(i)
                        if b + 1 < NB:
                            layer_norm(b + 1)
                        break
                    for t in range(2):
                        act.wait_ge(s_gst[t], b * (16 * TB // 2) + 16 * (h * JD // 2 + 1))
                    if h == 0:
                        act.wait_ge(s_out, b * (TB * 16) + 16)
                    for i in range(DH):
                        softplus(i)
                        if h:
                            tanh_z(i)
                        for n in FILL_AT[h][i]:
                            tanh_gate(n, n % 2)
                    act.wait_ge(s_dt, blk(b, h, DH))
                    if h:
                        act.wait_ge(s_af, a_use(b, DB + h * DH) + 2)
                    for i in range(DH):
                        decay(0, i)
                    tanh_gate(FILL - 1, (FILL - 1) % 2)
                    with act.Fori(0, DOWN // 2) as g:
                        for t in range(2):
                            n = 2 * g + t
                            for i in range(DH):
                                decay(n + 1, i)
                                if i == 2:
                                    tanh_gate(n + FILL, t)
                    for n in range(DOWN, NS):
                        for i in range(DH):
                            if n + 1 < NS:
                                decay(n + 1, i)
                            if i == 1 and n % 2 == 0 and n > DOWN:
                                tanh_down((n - DOWN) // 2 - 1)
                    tanh_down(JD - 1)

        @block.tensor
        def _(pe):
            give_credits(pe, "tensor")
            def layer_norm(b, tb):
                pe.wait_ge(s_xn, b * TB + tb + 1)
                pe.wait_ge(s_tact, t_use(b, tb) + 1)
                for k in range(HK):
                    mm = pe.transpose(psT[:, tb % 2, k * P:(k + 1) * P], yT[:, tb, k * P:(k + 1) * P], ident[:, :])
                mm.then_inc(s_tfa, 1)

            def in_proj(t, dst):
                for c in range(2):
                    for k in range(HK):
                        mm = pe.matmul(psA[:, dst, c * 512:(c + 1) * 512], w_is[:, t, k, :],
                                       xnT[:, k, c * 512:(c + 1) * 512], start=(k == 0), stop=(k == HK - 1))
                return mm

            def low_rank(it):
                if it < IT:
                    for gu in range(2):
                        use = 2 * it + gu
                        pe.wait_ge(s_lrr, use + 1)
                        at = (it * 2 + gu) * IM
                        for k in range(HK):
                            mm = pe.matmul(lr_bank(use)[:, k * IM:(k + 1) * IM],
                                           at_gu[:, gu * H + k * P:gu * H + (k + 1) * P], b_gu[:, at:at + IM],
                                           start=True, stop=True)
                        mm.then_inc(s_lr, 1)
                else:
                    use = IT + it
                    pe.wait_ge(s_lrr, use + 1)
                    at = (it - IT) * IM
                    pe.matmul(lr_bank(use)[0:IM, :], at_dn[:, at:at + IM], b_dn, start=True, stop=True).then_inc(s_lr, 1)

            pe.wait_ge(s_ident, 2)
            for tb in range(TB):
                layer_norm(0, tb)
            for b in range(NB):
                pe.wait_ge(s_tact, t_use(b, TB) + 2)

                def x_part(m):
                    pe.wait_ge(s_w[m % 2], landed(b, m))
                    pe.wait_ge(s_af, a_use(b, m) + 1)
                    in_proj(m % 2, m % 2).then_inc(s_wp, 1)

                def x_proj(k):
                    pe.wait_ge(s_xc, b * DB + k + 3)
                    for tb in range(TB):
                        mm = pe.matmul(psM[:, 0, tb * E:(tb + 1) * E], xc[:, k, tb * P:(tb + 1) * P], wx[:, k, :],
                                       start=(k == 0 and tb == 0), stop=(k == DB - 1 and tb == TB - 1))
                    return mm

                x_part(0)
                if b == 0:
                    pe.wait_ge(s_fc, 96)
                pe.wait_ge(s_wx, 16 * b + 16)
                pe.wait_ge(s_mf, b * M_USES + 2)
                for m in range(DB):
                    if m + 1 < DB:
                        x_part(m + 1)
                    if b == 0:
                        for it in range(PT * m, PT * (m + 1)):
                            low_rank(it)
                    if m > 0:
                        x_proj(m - 1)
                x_proj(DB - 1).then_inc(s_xp, 1)
                if b == 0:
                    pe.wait_ge(s_lrr, LR_USES + 3)
                pe.wait_ge(s_sn, b + 1)
                for t in range(2):
                    pe.wait_ge(s_tact, t_use(b, TB + t) + 1)
                    after_wait(pe)
                    for a in range(TB // 2):
                        mm = pe.transpose(psT[0:E, t, a * P:(a + 1) * P], ssm[:, t * TB // 2 + a, :], ident[:, :])
                    mm.then_inc(s_tfa, 1)
                pe.wait_ge(s_tact, t_use(b, TB + 2) + 2)

                for h in range(HALVES + 1):
                    def dt_proj(i):
                        if i == 0:
                            pe.wait_ge(s_wdt, b * 48 + 16 + 32 * h)
                            pe.wait_ge(s_af, a_use(b, DB) + 2)
                            if h:
                                pe.wait_ge(s_scan, unit(b, h, 0, 0) + 2)
                        elif h or i > 1:
                            pe.wait_ge(s_dtr, blk(b, h, i) if h else blk(b, h, i - 1))
                        m = (h * DH + i) * P
                        for c in range(2):
                            mm = pe.matmul(psA[:, dt_buf(h, i), c * 512:(c + 1) * 512], wdt[:, m:m + P],
                                           ssT[0:R, c * 512:(c + 1) * 512], start=True, stop=True)
                        mm.then_inc(s_dtp, 1)

                    def back_and_z(i):
                        off = w_z(h - 1, i)
                        pe.wait_ge(s_tdve, t_group(b, h, 0, 0) + 2)
                        pe.wait_ge(s_ybr, blk(b, h - 1, i) + 1)
                        for tb in range(TB):
                            mm = pe.transpose(psT[:, tb // 4, tb % 4 * P:(tb % 4 + 1) * P],
                                              yT[:, tb, i * P:(i + 1) * P], ident[:, :])
                        mm.then_inc(s_yb, 1)
                        pe.wait_ge(s_w[off % 2], landed(b, off))
                        pe.wait_ge(s_af, a_use(b, DB + (h - 1) * DH + i) + 2)
                        if i == 0:
                            pe.wait_ge(s_scan, unit(b, h, 0, 0) + 2)
                        in_proj(off % 2, 1).then_inc(s_wp, 1)

                    def turn(n, t, tb):
                        if tb == 0:
                            pe.wait_ge(s_scan, unit(b, h, n, DH) + 2)
                            if h:
                                pe.wait_ge(s_ybr, blk(b, h, 0) + 1)
                        pe.wait_ge(s_tdve, t_group(b, h, n, tb) + 1)
                        for i in range(DH):
                            mm = pe.transpose(psT[:, tb % 2, i * P:(i + 1) * P],
                                              hb[:, t * DH + i, tb * P:(tb + 1) * P], ident[:, :])
                        mm.then_inc(s_tfd, 1)

                    def gate_up(n, t, q, land):
                        gu = q // 2
                        if q == 0:
                            pe.wait_ge(s_w[t], land)
                        if q % 2 == 0:
                            pe.wait_ge(s_mf, m_half(b, h, 2 * n + gu) + 1)
                        for k in range(2 * (q % 2), 2 * (q % 2) + 2):
                            at = (gu * HK + k) * IM
                            mm = pe.matmul(psM[0:IM, gu, :], w_ts[:, t, at:at + IM],
                                           xnT[:, k, h * CH:(h + 1) * CH], start=(k == 0), stop=(k == HK - 1))
                        if q % 2 == 1:
                            mm.then_inc(s_fg if gu == 0 else s_wp, 1)

                    def down(j, q):
                        if q == 0:
                            pe.wait_ge(s_mf, m_half(b, h, 2 * IT + j) + 1)
                        if q == 7 and j == 0:
                            pe.wait_ge(s_mf, m_half(b, h, 2 * IT - 1) + 3)
                        for k in range(IT * q // 8, IT * (q + 1) // 8):
                            mm = pe.matmul(psM[:, j % 2, :], hid[0:IM, k, j * P:(j + 1) * P], w_dn[0:IM, k, :],
                                           start=(k == 0), stop=(k == IT - 1))
                        if q == 7:
                            mm.then_inc(s_fd, 1)

                    if h == HALVES:
                        for i in range(DH):
                            back_and_z(i)
                        break
                    for i in range(DH):
                        dt_proj(i)
                        if h:
                            back_and_z(i)
                        for n in FILL_AT[h][i] + [FILL - 1] * (i == DH - 1):
                            off = w_g(h, n)
                            for q in range(4):
                                gate_up(n, off % 2, q, landed(b, off))
                    with pe.Fori(0, DOWN // 2) as g:
                        for t in range(2):
                            for q in range(4):
                                turn(2 * g + t, t, 2 * q)
                                turn(2 * g + t, t, 2 * q + 1)
                                gate_up(2 * g + (FILL + t), t, q, landed(b, w_g(h, FILL)) + 16 * g)
                    for n in range(DOWN, NS):
                        for q in range(4):
                            turn(n, n % 2, 2 * q)
                            turn(n, n % 2, 2 * q + 1)
                            down((n - DOWN) // 2, 4 * (n % 2) + q)
                pe.wait_ge(s_wo, 16 * b + 16)
                pe.wait_ge(s_y, DB * b + DB + 1)
                if b + 1 < NB:
                    pe.wait_ge(s_ybr, blk(b, HALVES, 0) + 1)
                for tb in range(TB):
                    if b + 1 < NB and tb >= TB // 2:
                        layer_norm(b + 1, 2 * tb - TB)
                        layer_norm(b + 1, 2 * tb - TB + 1)
                    pe.wait_ge(s_mf, m_half(b, HALVES, 0) + tb + 1)
                    for k in range(DB):
                        mm = pe.matmul(psM[:, tb % 2, :], xc[:, k, tb * P:(tb + 1) * P], hid[:, k, :],
                                       start=(k == 0), stop=(k == DB - 1))
                    mm.then_inc(s_sp, 1)

        @block.vector
        def _(dve):
            give_credits(dve, "vector")
            def stt(out, in0, scalar, in1, op0, op1):
                return dve.scalar_tensor_tensor(out=out, in0=in0, scalar=scalar, in1=in1, op0=op0, op1=op1)

            psT_row = psT[:, :, :].rearrange("p a c -> p (a c)")
            def statistics(b):
                dve.wait_ge(s_x, 16 * b + 16)
                for tb in range(TB):
                    dve.bn_stats(st[:, tb, :], yT[:, tb, :]).then_inc(s_st, 1)
                for tb in range(TB):
                    dve.wait_ge(s_st, b * TB + tb + 1)
                    dve.bn_aggr(mv[:, tb, :], st[:, tb, :]).then_inc(s_mv, 1)

            def scale_shift(b):
                dve.wait_ge(s_std, b + 1)
                dve.reciprocal(rs[:, :], rs[:, :]).then_inc(s_rstd, 1)
                dve.wait_ge(s_rstd, b + 1)
                stt(nm[:, :], mv[:, :, 0], -1.0, rs[:, :], ALU.mult, ALU.mult).then_inc(s_nm, 1)

            def ffn_weights(it):
                t = it % 2
                dve.wait_ge(s_q[t], 16 * (it // 2) + 16)
                if it < IT:
                    dve.wait_ge(s_wst[t], 16 * (it // 2) + 16)
                    for gu in range(2):
                        sl = slice(gu * HK * IM, (gu + 1) * HK * IM)
                        at = (2 * it + gu) * IM
                        scale = scales[:, at:at + IM].rearrange("p (k i) -> p k i", k=1).to_broadcast([P, HK, IM])
                        ins = stt(wf[:, t, sl].rearrange("p (k i) -> p k i", k=HK),
                                  qs[:, t, sl].rearrange("p (k i) -> p k i", k=HK), -Q_ZERO, scale, ALU.add, ALU.mult)
                    ins.then_inc(s_deq, 1)
                    dve.wait_ge(s_deq, it + 3)
                    for gu in range(2):
                        use = 2 * it + gu
                        w = wf[:, t, gu * HK * IM:(gu + 1) * HK * IM]
                        dve.wait_ge(s_lr, use + 1)
                        stt(w, lr_bank(use)[:, 0:HK * IM], LR_SCALE, w, ALU.mult, ALU.add).then_inc(s_lrr, 1)
                else:
                    use = IT + it
                    w = w_dn[0:IM, it - IT, :]
                    stt(w, qs[0:IM, t, 0:H], -Q_ZERO, scales[0:IM, 2 * IT * IM:], ALU.add, ALU.mult).then_inc(s_deq, 1)
                    dve.wait_ge(s_deq, it + 3)
                    dve.wait_ge(s_lr, use + 1)
                    stt(w, lr_bank(use)[0:IM, :], LR_SCALE, w, ALU.mult, ALU.add).then_inc(s_lrr, 1)

            psT_row = psT[:, :, :].rearrange("p a c -> p (a c)")
            statistics(0)
            dve.wait_ge(s_const, 32)
            dve.tensor_scalar(hc, hc, 0.5, None, ALU.mult).then_inc(s_prep, 1)
            dve.wait_ge(s_negA, 1)
            dve.tensor_scalar(negA, negA, -1.0, None, ALU.mult).then_inc(s_prep, 1)
            scale_shift(0)
            dve.wait_ge(s_fc, 96)
            dve.tensor_scalar(scales, scales, Q_STEP, None, ALU.mult).then_inc(s_scl, 1)
            dve.wait_ge(s_scl, 1)

            for b in range(NB):
                def conv(m, t):
                    dve.wait_ge(s_acc, b * DB + m + 1)
                    for k in range(KC - 2, -1, -1):
                        lag = KC - 1 - k
                        if k < KC - 2:
                            dve.wait_ge(s_tap, b * (2 * DB) + 2 * m + lag - 1)
                        ins = stt(tmp[:, t, lag:L], psA[:, t, 0:L - lag], hc[:, m, k:k + 1], tmp[:, t, lag:L],
                                  ALU.mult, ALU.add)
                        ins.then_inc(s_tap if k else s_af, 1)

                def conv_silu(m, t):
                    dve.wait_ge(s_thc, b * DB + m + 1)
                    stt(xc[:, m, :], tmp[:, 2 + t, :], 1.0, tmp[:, t, :], ALU.add, ALU.mult).then_inc(s_xc, 1)

                for m in range(DB):
                    conv(m, m % 2)
                    if b == 0:
                        ffn_weights(PT * m)
                    conv_silu(m, m % 2)
                    if b == 0:
                        for j in range(1, PT):
                            ffn_weights(PT * m + j)
                dve.wait_ge(s_sq, b + 1)
                dve.tensor_reduce(ms[:, :, 0:1], sq[:, :, 0:R], AX.X, ALU.add).then_inc(s_ms, 1)
                dve.tensor_reduce(ms[:, :, 1:3], sq[:, :, R:E].rearrange("p a (g n) -> p a g n", g=2), AX.X,
                                  ALU.add).then_inc(s_ms, 1)
                dve.wait_ge(s_rms, 2 * b + 2)
                dve.reciprocal(ms[:, :, :], ms[:, :, :]).then_inc(s_rinv, 1)
                dve.wait_ge(s_rinv, b + 1)
                dve.wait_ge(s_xpr, b + 1)
                for g, (lo, hi) in enumerate([(0, R), (R, R + NS), (R + NS, E)]):
                    dve.tensor_tensor(ssm[:, :, lo:hi], ssm[:, :, lo:hi],
                                      ms[:, :, g:g + 1].to_broadcast([P, TB, hi - lo]), ALU.mult).then_inc(s_sn1, 1)
                dve.wait_ge(s_sn1, 3 * b + 3)
                dve.tensor_tensor(ssm[:, :, :], ssm[:, :, :],
                                  lnw[:, :].rearrange("p (a e) -> p a e", a=1).to_broadcast([P, TB, E]), ALU.mult
                                  ).then_inc(s_sn, 1)

                for h in range(HALVES + 1):
                    def softplus(i):
                        k = blk(b, h, i)
                        e, w = soft_tmp(i)
                        dve.wait_ge(s_e1, k + 1)
                        stt(tmp[:, e, :], tmp[:, w, :], -1.0, tmp[:, e, :], ALU.add, ALU.subtract).then_inc(s_nd, 1)
                        dve.wait_ge(s_nd, k + 1)
                        dve.wait_ge(s_ln, k + 1)
                        dve.tensor_tensor(tmp[:, e, :], tmp[:, w, :], tmp[:, e, :], ALU.subtract).then_inc(s_rl, 1)
                        dve.wait_ge(s_rl, k + 1)
                        dve.tensor_tensor(dt[:, i, :], dt[:, i, :], tmp[:, e, :], ALU.add).then_inc(s_dt, 1)

                    def add_dx(i):
                        k, m = blk(b, h - 1, i), (h - 1) * DH + i
                        dve.wait_ge(s_yb, k + 1)
                        stt(xc[:, m, :], xc[:, m, :], cc[:, m, DP:DP + 1], psT_row, ALU.mult, ALU.add).then_inc(s_ybr, 1)

                    def gate_z(i):
                        k, m, v = blk(b, h - 1, i), (h - 1) * DH + i, tmp[:, i % 2, :]
                        dve.wait_ge(s_thz, k + 1)
                        stt(v, v, 1.0, psA[:, 1, :], ALU.add, ALU.mult).then_inc(s_af, 1)
                        dve.wait_ge(s_ybr, k + 2)
                        dve.wait_ge(s_af, a_use(b, DB + (h - 1) * DH + i) + 3)
                        stt(xc[:, m, :], xc[:, m, :], 0.5, v, ALU.mult, ALU.mult).then_inc(s_y, 1)

                    def scan(n, t, i):
                        dve.wait_ge(s_a, unit(b, h, n, i) + 1)
                        dve.wait_ge(s_u, unit(b, h, n, i) + 9)
                        dve.tensor_tensor_scan(hb[:, t * DH + i, :], psA[:, i % 2, :], ub[:, i % 2, :], 0.0,
                                               ALU.mult, ALU.add).then_inc(s_scan, 1)

                    def add_y(n, tb, first):
                        dve.wait_ge(s_tfd, t_group(b, h, n, tb) + 1)
                        if not first:
                            dve.wait_ge(s_tdve, t_group(b, h, n - 1, tb) + 3)
                        stt(yT[:, tb, :], psT[:, tb % 2, :], ssm[:, tb, bass.ds(n + (R + NS), 1)], yT[:, tb, :],
                            ALU.mult, ALU.add).then_inc(s_tdve, 1)

                    def silu_gate(n, t):
                        dve.wait_ge(s_th, b * (HALVES * NS) + h * NS + n + 1)
                        stt(th[0:IM, t, :], th[0:IM, t, :], 1.0, psM[0:IM, 0, :], ALU.add, ALU.mult).then_inc(s_mf, 1)

                    def hidden(n, t):
                        dve.wait_ge(s_wp, w_use(b, w_g(h, n) if isinstance(n, int) else n + (w_g(h, FILL) - FILL)) + 3)
                        dve.wait_ge(s_mf, m_half(b, h, 2 * n) + 3)
                        stt(hid[0:IM, n, :], th[0:IM, t, :], 0.5, psM[0:IM, 1, :], ALU.mult, ALU.mult).then_inc(s_mf, 1)

                    def silu_down(j):
                        dve.wait_ge(s_th, b * (HALVES * NS) + (h * NS + IT + j + 1))
                        stt(th[:, j % 2, :], th[:, j % 2, :], 1.0, psM[:, j % 2, :], ALU.add, ALU.mult).then_inc(s_mf, 1)

                    def slot(n, t, first=False, last=False, gate=None, up=None, dn=None):
                        for i in range(DH):
                            if not last:
                                scan(n + 1, 1 - t, i)
                            add_y(n, 2 * i, first)
                            if i == DH - 1 and gate is not None:
                                silu_gate(gate, t)
                            add_y(n, 2 * i + 1, first)
                            if i == 0 and up is not None:
                                hidden(up, 1 - t)
                            if i == 1 and dn is not None:
                                silu_down(dn)

                    if h == HALVES:
                        for i in range(DH):
                            add_dx(i)
                            gate_z(i)
                        break
                    for i in range(DH):
                        if h:
                            add_dx(i)
                        softplus(i)
                        if h:
                            gate_z(i)
                        for n in FILL_AT[h][i]:
                            silu_gate(n, n % 2)
                            hidden(n, n % 2)
                    dve.wait_ge(s_yz, b * HALVES + h + 1)
                    for i in range(DH):
                        scan(0, 0, i)
                    silu_gate(FILL - 1, (FILL - 1) % 2)
                    slot(0, 0, first=True, gate=FILL, up=FILL - 1)
                    with dve.Fori(0, DOWN // 2 - 1) as g:
                        slot(2 * g + 1, 1, gate=2 * g + (FILL + 1), up=2 * g + FILL)
                        slot(2 * g + 2, 0, gate=2 * g + (FILL + 2), up=2 * g + (FILL + 1))
                    slot(DOWN - 1, 1, gate=IT - 1, up=IT - 2)
                    slot(DOWN, 0, up=IT - 1)
                    for n in range(DOWN + 1, NS):
                        slot(n, n % 2, last=(n == NS - 1), dn=None if n % 2 else (n - DOWN) // 2 - 1)
                    silu_down(JD - 1)
                dve.wait_ge(s_xg, 32 * b + 32)
                for tb in range(TB):
                    dve.wait_ge(s_sp, b * TB + tb + 1)
                    stt(gt[:, tb, :], psM[:, tb % 2, :], 0.5, gt[:, tb, :], ALU.mult, ALU.mult).then_inc(s_mf, 1)
                    if b + 1 < NB and tb == 0:
                        statistics(b + 1)
                    if b + 1 < NB and tb == 1:
                        scale_shift(b + 1)


def kernel(**inputs):
    import concourse.bacc as bacc
    from concourse.bass_utils import run_bass_kernel_spmd

    def arr(name):
        return np.asarray(inputs[name])

    def pad(a, axis):
        width = [(0, 0)] * a.ndim
        width[axis] = (0, IT * IM - I)
        return np.pad(a, width)

    def per_channel(a):
        return a.reshape(DB, P, -1).transpose(1, 0, 2)

    def ffn_in(q):
        return pad(q, 0).reshape(IT, IM, HK, P).transpose(0, 3, 2, 1)

    A, F = "L0_attn_", "L0_ffn_"
    gu = ("gate", "up")
    data = {
        "x": arr(A + "hidden_states"),
        "w_in": arr(A + "in_proj_w").reshape(HK, P, 2 * DB, P).transpose(2, 1, 0, 3),
        "chan": np.concatenate([per_channel(arr(A + n)) for n in ("conv_w", "conv_b", "dt_bias", "D_param", "A_log")], 2),
        "w_x": per_channel(arr(A + "x_proj_w").T),
        "w_dt": arr(A + "dt_proj_w").T,
        "ln_w": np.concatenate([arr(A + n) for n in ("dt_ln_w", "B_ln_w", "C_ln_w")])[None],
        "w_out": per_channel(arr(A + "out_proj_w").T),
        "gu_q": np.stack([ffn_in(arr(F + n + "_q")) for n in gu], 2).reshape(IT, P, 2 * HK * IM),
        "gu_s": np.stack([pad(arr(F + n + "_scale"), 0).reshape(IT, IM) for n in gu], 1).reshape(1, -1),
        "gu_at": np.stack([arr(F + n + "_A").T for n in gu], 1),
        "gu_b": np.stack([pad(arr(F + n + "_B"), 1).reshape(R, IT, IM) for n in gu], 2).reshape(R, -1),
        "dn_q": pad(arr(F + "down_q").T, 0).reshape(IT, IM, H),
        "dn_s": arr(F + "down_scale")[None],
        "dn_at": pad(arr(F + "down_A"), 0).T,
        "dn_b": arr(F + "down_B"),
    }
    data = {f"{n}_dram": np.ascontiguousarray(a) for n, a in data.items()}
    nc = bacc.Bacc("TRN2", target_bir_lowering=False, num_devices=1)
    args = [nc.dram_tensor(n, a.shape, mybir.dt.from_np(a.dtype), kind="ExternalInput").ap() for n, a in data.items()]
    args.append(nc.dram_tensor("out_dram", (NB, L, H), F32, kind="ExternalOutput").ap())
    build(nc, *args)
    r = run_bass_kernel_spmd(nc, [data], core_ids=[0])
    return r.results[0]["out_dram"]
```

```python
from contextlib import ExitStack

import numpy as np

import concourse.bass as bass
from concourse import mybir

F32 = mybir.dt.float32
I32 = mybir.dt.int32
ALU = mybir.AluOpType
ACT = mybir.ActivationFunctionType
AX = mybir.AxisListType

P = 128
NB, L, H = 2, 1024, 512
D, NS, R, KC = 1024, 16, 32, 4
E = R + 2 * NS
I = 1376
IT = 11
IM = 126
HK, DB, TB = H // P, D // P, L // P
HALVES, DH = 2, DB // 2
CH = L // HALVES
JD = CH // P
LN_EPS, RMS_EPS = 1e-5, 1e-6
Q_ZERO, Q_STEP, LR_SCALE = 7.5, 0.005, 0.02
CW, CB, DTB, DP, AL = 0, KC, KC + 1, KC + 2, KC + 3
NCC = AL + NS

W_HALF = IT + DH
W_USES = DB + HALVES * W_HALF
FILL = 3
LATE = IT - FILL
STEPS = [("z", i, s) for i in range(DH) for s in range(2 * HK)] + [("d", j, s) for j in range(CH // P)
                                                                  for s in range(IT)]
QUARTERS = 4 * (NS - LATE)


def steps_of(p):
    return STEPS[len(STEPS) * p // QUARTERS:len(STEPS) * (p + 1) // QUARTERS]


def ends(p):
    done = []
    for kind, i, s in steps_of(p):
        if kind == "z" and s % HK == HK - 1:
            done.append(("z", i, s // HK))
        if kind == "d" and s == IT - 1:
            done.append(("d", i, 0))
    return done


SP_LATE = [("Z", 0), ("Z", 1), ("B", 10), ("z", 0, 0), ("Z", 2), ("z", 0, 1), ("B", 11),
           ("z", 1, 0), ("Z", 3), ("z", 1, 1), ("B", 12), ("z", 2, 0), ("z", 2, 1), ("B", 13), ("z", 3, 0),
           ("z", 3, 1), ("G", 0), ("G", 1), ("B", 14), ("d", 0, 0), ("B", 15), ("d", 1, 0), ("back",), ("W",), ("d", 2, 0), ("w",),
           ("d", 3, 0)]

T_ACT = TB + 2
T_DVE = HALVES * NS * TB
LR_USES = 3 * IT
QD = 3
PT = 3
A_USES = DB
M_HALF = 2 * IT + 2 * DH + JD
TH_HALF = DH + JD // 2
M_USES = HALVES * M_HALF + TB


def build(nc, x, w_in, chan, w_x, w_dt, ln_w, w_out, gu_q, gu_s, gu_at, gu_b, dn_q, dn_s, dn_at, dn_b, out):
    ctx = ExitStack()
    with ctx:
        def sb(name, shape, dt=F32):
            return ctx.enter_context(nc.sbuf_tensor(name, shape, dt))

        def sem(name):
            return ctx.enter_context(nc.semaphore(name))

        w_gu = nc.dram_tensor("w_gu_scratch", [IT, P, 2 * HK * IM], F32).ap()
        ss_rows = nc.dram_tensor("ss_rows_scratch", [NB, E, L], F32).ap()
        z_rows = nc.dram_tensor("z_scratch", [NB, DB, P, L], F32).ap()
        g_rows = nc.dram_tensor("g_scratch", [NB, L, H], F32).ap()

        xnT = sb("xnT", [P, HK, L])
        xc = sb("xc", [P, DB, L])
        dt = sb("dt", [P, DH, L])
        dtx = sb("dtx", [P, DH, L])
        yT = sb("yT", [P, TB, DH * P])
        hb = sb("hb", [P, 2 * DH, L])
        ub = sb("ub", [P, 2, L])
        bn = sb("bn", [P, 2, L])
        hid = sb("hid", [P, IT, CH])
        w_dn = sb("w_dn", [P, IT, H])
        w_ts = sb("w_ts", [P, 2, 2 * HK * IM])
        th = sb("th", [P, 2, CH])
        ident = sb("ident", [P, P])
        cc = sb("cc", [P, DB, NCC])
        lnw = sb("lnw", [P, E])
        st = sb("st", [P, TB, 6])
        mv = sb("mv", [P, TB, 2])
        rs = sb("rs", [P, TB])
        nm = sb("nm", [P, TB])
        ssm = sb("ssm", [P, TB, E])
        ms = sb("ms", [P, TB, 3])
        tmp = hb
        wx = hb[:, DH, 0:DB * E].rearrange("p (k e) -> p k e", e=E)
        ssT = hb[0:E, DH + 1, :]
        wdt = hb[0:R, DH + 2, 0:D]
        sq = hb[:, DH + 3, 0:TB * E].rearrange("p (a e) -> p a e", e=E)
        w_o = dt[:, :, :].rearrange("p i (s c) -> p (i s) c", c=H)
        xt = hid[:, 0:TB, :]
        gt = dtx[:, :, :].rearrange("p i (s c) -> p (i s) c", c=H)
        hid_flat = hid[:, :, :].rearrange("p a c -> p (a c)")
        dt_flat = dt[:, :, :].rearrange("p a c -> p (a c)")
        dtx_flat = dtx[:, :, :].rearrange("p a c -> p (a c)")
        WT = 2 * HK * IM
        wf = hid_flat[:, 0:QD * WT].rearrange("p (t c) -> p t c", t=QD)
        qs = [a[:, t, 0:WT].bitcast(I32) for a in (ub, bn) for t in range(2)]
        at_gu = hid_flat[0:R, QD * WT:QD * WT + 2 * H]
        at_dn = hid_flat[0:R, QD * WT + 2 * H:QD * WT + 2 * H + IT * IM]
        b_gu = dtx_flat[0:R, 0:2 * IT * IM]
        b_dn = dtx_flat[0:R, 2 * IT * IM:2 * IT * IM + H]
        scales = dt_flat[:, 0:2 * IT * IM + H]
        w_is = w_ts[:, :, 0:HK * P].rearrange("p t (k j) -> p t k j", k=HK)
        hc = cc[:, :, CW:CB + 1]
        negA = cc[:, :, AL:AL + NS]

        psA = ctx.enter_context(nc.psum_tensor("psA", [P, 2, L], F32))
        psT = ctx.enter_context(nc.psum_tensor("psT", [P, 2, 512], F32))
        psM = ctx.enter_context(nc.psum_tensor("psM", [P, 2, 512], F32))

        s_past = sem("s_past")
        s_const = sem("s_const")
        s_fc = sem("s_fc")
        s_ident = sem("s_ident")
        s_negA = sem("s_negA")
        s_prep = sem("s_prep")
        s_q = [sem(f"s_q{t}") for t in range(QD)]
        s_scl = sem("s_scl")
        s_lr = sem("s_lr")
        s_deq = sem("s_deq")
        s_lrr = sem("s_lrr")
        s_wst = [sem(f"s_wst{t}") for t in range(QD)]
        s_x = sem("s_x")
        s_st = sem("s_st")
        s_mv = sem("s_mv")
        s_std = sem("s_std")
        s_rstd = sem("s_rstd")
        s_nm = sem("s_nm")
        s_xn = sem("s_xn")
        s_tact = sem("s_T_act")
        s_tdve = sem("s_T_dve")
        s_tfa = sem("s_Ta_full")
        s_tfd = sem("s_Td_full")
        s_af = sem("s_A_free")
        s_mf = sem("s_M_free")
        s_w = [sem("s_w0"), sem("s_w1")]
        s_wp = sem("s_wp")
        s_acc = sem("s_acc")
        s_tap = sem("s_tap")
        s_thc = sem("s_thc")
        s_xc = sem("s_xc")
        s_wx = sem("s_wx")
        s_wdt = sem("s_wdt")
        s_xp = sem("s_xp")
        s_xpr = sem("s_xpr")
        s_sq = sem("s_sq")
        s_ms = sem("s_ms")
        s_rms = sem("s_rms")
        s_rinv = sem("s_rinv")
        s_sn1 = sem("s_sn1")
        s_sn = sem("s_sn")
        s_bst = sem("s_bst")
        s_dtp = sem("s_dtp")
        s_dtr = sem("s_dtr")
        s_abs = sem("s_abs")
        s_e = sem("s_e")
        s_e1 = sem("s_e1")
        s_ln = sem("s_ln")
        s_nd = sem("s_nd")
        s_rl = sem("s_rl")
        s_dt = sem("s_dt")
        s_dtx = sem("s_dtx")
        s_dtxp = sem("s_dtxp")
        s_B = [sem("s_B0"), sem("s_B1")]
        s_u = sem("s_u")
        s_a = sem("s_a")
        s_scan = sem("s_scan")
        s_fg = sem("s_fg")
        s_fd = sem("s_fd")
        s_th = sem("s_th")
        s_ths = [sem("s_ths0"), sem("s_ths1")]
        s_yb = sem("s_yb")
        s_ybr = sem("s_ybr")
        s_zl = sem("s_zl")
        s_y = sem("s_y")
        s_wo = sem("s_wo")
        s_xg = sem("s_xg")
        s_gl = sem("s_gl")
        s_sp = sem("s_sp")
        s_o = sem("s_o")
        s_out = sem("s_out")
        CREDITS = {
            "vector": [(s_tdve, 2), (s_af, 2), (s_mf, 2), (s_deq, QD), (s_lrr, 3), (s_xc, 2), (s_scan, 2),
                       (s_y, 1), (s_ybr, 1)],
            "scalar": [(s_tact, 2)] + [(s, 16) for s in s_wst],
            "tensor": [(s_wp, 2)],
            "gpsimd": [(s_u, 8)],
            "sync": [(s_ths[0], 16), (s_ths[1], 16), (s_out, 16)],
        }

        def t_use(b, j):
            return b * T_ACT + j

        def t_group(b, h, n, tb):
            return b * T_DVE + h * (NS * TB) + n * TB + tb

        def a_use(b, j):
            return b * A_USES + j

        def w_use(b, off):
            return b * W_USES + off

        def landed(b, off):
            return b * (8 * W_USES) + 16 * (off // 2 + 1)

        def w_half(h, n):
            return DB + h * W_HALF + n

        def m_half(b, h, j):
            return b * M_USES + h * M_HALF + j

        def unit(b, h, n, i):
            return b * (HALVES * NS * DH) + h * NS * DH + n * DH + i

        def fg_use(b, h, n):
            return b * (HALVES * W_HALF) + h * W_HALF + n

        def m_late(b, h, kind, i, c):
            return m_half(b, h, 2 * IT + (2 * i + c if kind == "z" else 2 * DH + i))

        def th_done(b, h, kind, i, c):
            return (b * HALVES + h) * (IT + 2 * DH + JD) + IT + (2 * i + c if kind == "z" else 2 * DH + i) + 1

        def th_stored(b, h, n):
            return 16 * ((b * HALVES + h) * TH_HALF + n + 2)

        def soft_tmp(i):
            return (hb[:, DH, :], hb[:, DH + 3, :]) if i % 2 else (ub[:, 0, :], ub[:, 1, :])

        def blk(b, h, i):
            return b * DB + h * DH + i

        def lr_uses(m):
            return min(PT * m, 2 * IT) + min(PT * m, IT)

        def lr_bank(use):
            return psM[:, 1, :] if use % 3 == 0 else psT[:, use % 3 - 1, :]

        def b_loads(b, h, pair):
            return b * (16 * HALVES * NS // 2) + (16 * (h * NS // 2 + 1)) + pair * 16

        def give_credits(engine, name):
            for s, n in CREDITS[name]:
                engine.sem_inc(s, n)

        def after_wait(engine):
            engine.sem_inc(s_past, 1)

        block = ctx.enter_context(nc.Block())

        @block.sync
        def _(sp):
            give_credits(sp, "sync")
            def load_x(b):
                sp.dma_start(yT[:, :, :], x[b].rearrange("(a p) h -> p a h", p=P)).then_inc(s_x, 16)

            def load_small():
                sp.dma_start(wx, w_x).then_inc(s_wx, 16)
                sp.dma_start(wdt, w_dt).then_inc(s_wdt, 16)

            def load_w_in(b, m):
                sp.wait_ge(s_wp, w_use(b, m) + 1)
                sp.dma_start(w_is[:, m % 2, :, :], w_in[m]).then_inc(s_w[m % 2], 16)

            def load_q(it):
                t = it % QD
                sp.wait_ge(s_deq, it + 1)
                if it < IT:
                    sp.dma_start(qs[t], gu_q[it]).then_inc(s_q[t], 16)
                else:
                    sp.dma_start(qs[t][0:IM, 0:H], dn_q[it - IT]).then_inc(s_q[t], 16)

            load_x(0)
            sp.dma_start(cc[:, :, :], chan).then_inc(s_const, 16)
            sp.dma_start(lnw[:, :], ln_w.to_broadcast([P, E])).then_inc(s_const, 16)
            load_w_in(0, 0)
            sp.dma_start(scales[:, 0:2 * IT * IM], gu_s.to_broadcast([P, 2 * IT * IM])).then_inc(s_fc, 16)
            sp.dma_start(scales[:, 2 * IT * IM:], dn_s.to_broadcast([P, H])).then_inc(s_fc, 16)
            load_q(0)
            load_w_in(0, 1)
            for it in range(1, QD):
                load_q(it)
            sp.dma_start(at_gu, gu_at.rearrange("r g h -> r (g h)")).then_inc(s_fc, 16)
            sp.dma_start(b_gu, gu_b).then_inc(s_fc, 16)
            sp.dma_start(at_dn, dn_at).then_inc(s_fc, 16)
            sp.dma_start(b_dn, dn_b).then_inc(s_fc, 16)
            load_small()

            for b in range(NB):
                for m in range(DB):
                    if m + 2 < DB:
                        load_w_in(b, m + 2)
                    if b == 0:
                        for it in range(PT * m + QD, min(PT * (m + 1) + QD, 2 * IT)):
                            load_q(it)
                def load_g(n, off, t):
                    sp.wait_ge(s_wp, w_use(b, off) + 1)
                    sp.dma_start(w_ts[:, t, :], w_gu[n]).then_inc(s_w[t], 16)

                if b == 0:
                    for t in range(QD):
                        sp.wait_ge(s_wst[t], 16 + 16 * len(range(t, IT, QD)))
                for t in range(2):
                    load_g(t, w_half(0, t), t)
                sp.wait_ge(s_tact, t_use(b, TB + 2) + 2)
                sp.dma_start(ss_rows[b], ssT).then_inc(s_bst, 16)
                sp.wait_ge(s_bst, 16 * b + 16)
                after_wait(sp)

                for h in range(HALVES):
                    def load_b(n, t):
                        sp.wait_ge(s_u, unit(b, h, n, 0) + 4)
                        sp.dma_start(bn[:, t, :], ss_rows[b, bass.ds(n + R, 1), :].to_broadcast([P, L])).then_inc(s_B[t], 16)

                    def load_z(i):
                        off = w_half(h, IT + i)
                        sp.wait_ge(s_wp, w_use(b, off) + 1)
                        sp.dma_start(w_is[:, off % 2, :, :], w_in[DB + h * DH + i]).then_inc(s_w[off % 2], 16)

                    def store(kind, i, c):
                        t = c if kind == "z" else i % 2
                        sp.wait_ge(s_mf, m_late(b, h, kind, i, c) + 3)
                        if kind == "z":
                            place = z_rows[b, h * DH + i, :, c * CH:(c + 1) * CH]
                        else:
                            place = g_rows[b, (h * JD + i) * P:(h * JD + i + 1) * P, :]
                        sp.dma_start(place, th[:, t, :]).then_inc(s_ths[t], 16)

                    for t in range(2):
                        load_b(t, t)
                    for n in range(2, FILL):
                        load_g(n, w_half(h, n), w_half(h, n) % 2)
                    with sp.Fori(0, LATE // 2) as g:
                        for t in range(2):
                            load_g(2 * g + (FILL + t), 2 * g + (w_half(h, FILL) + t), (w_half(h, FILL) + t) % 2)
                            load_b(2 * g + (2 + t), t)
                    for what in SP_LATE:
                        if what[0] == "B":
                            load_b(what[1], what[1] % 2)
                        elif what[0] == "Z":
                            load_z(what[1])
                        elif what[0] == "G":
                            if h + 1 < HALVES:
                                load_g(what[1], w_half(h + 1, what[1]), w_half(h + 1, what[1]) % 2)
                        elif what[0] == "back":
                            sp.wait_ge(s_tfd, t_group(b, h, NS - 1, 0))
                            for t in range(2):
                                sp.wait_ge(s_ths[t], th_stored(b, h, DH - 1))
                            for i in range(DH):
                                sp.dma_start(hb[:, i, :], z_rows[b, h * DH + i]).then_inc(s_zl, 16)
                        elif what[0] == "w":
                            if h + 1 < HALVES:
                                sp.wait_ge(s_tfd, t_group(b, h, NS, 0))
                                sp.dma_start(wdt, w_dt).then_inc(s_wdt, 16)
                                sp.dma_start(ssT[0:R, :], ss_rows[b, 0:R, :]).then_inc(s_wdt, 16)
                        elif what[0] == "W":
                            if h + 1 == HALVES:
                                sp.wait_ge(s_a, unit(b, HALVES, 0, 0))
                                sp.dma_start(w_o, w_out).then_inc(s_wo, 16)
                        else:
                            store(*what)

                sp.wait_ge(s_u, unit(b, HALVES, 0, 0) + 8)
                for t in range(2):
                    sp.wait_ge(s_ths[t], th_stored(b, HALVES - 1, TH_HALF - 1))
                sp.dma_start(gt, g_rows[b].rearrange("(a p) h -> p a h", p=P)).then_inc(s_gl, 16)
                sp.wait_ge(s_fd, b * TB + TB)
                sp.dma_start(xt, x[b].rearrange("(a p) h -> p a h", p=P)).then_inc(s_xg, 16)
                if b + 1 < NB:
                    sp.wait_ge(s_tfd, t_group(b, HALVES, 0, 0))
                    load_small()
                    sp.wait_ge(s_yb, blk(b, HALVES, 0))
                    load_x(b + 1)
                    load_w_in(b + 1, 0)
                    load_w_in(b + 1, 1)
                with sp.Fori(0, TB) as tb:
                    sp.wait_ge(s_o, b * TB + tb + 1)
                    sp.dma_start(out[b, bass.ts(tb, P), :], xt[:, tb, :]).then_inc(s_out, 16)
            sp.wait_ge(s_out, NB * TB * 16 + 16)

        @block.gpsimd
        def _(pool):
            give_credits(pool, "gpsimd")
            pool.memset(ident[:, :], 0.0).then_inc(s_ident, 1)
            pool.wait_ge(s_ident, 1)
            pool.affine_select(out=ident[:, :], in_=ident[:, :], compare_op=ALU.not_equal, fill=1.0,
                               base=0, pattern=[[-1, P]], channel_multiplier=1).then_inc(s_ident, 1)
            def layer_norm(b):
                pool.wait_ge(s_nm, b + 1)
                after_wait(pool)
                for tb in range(TB):
                    pool.tensor_scalar(yT[:, tb, :], yT[:, tb, :], rs[:, tb:tb + 1], nm[:, tb:tb + 1],
                                       ALU.mult, ALU.add).then_inc(s_xn, 1)

            layer_norm(0)
            for b in range(NB):
                for h in range(HALVES):
                    for i in range(DH - 1):
                        k = blk(b, h, i)
                        pool.wait_ge(s_dt, k + 1)
                        pool.tensor_tensor(dtx[:, i, :], dt[:, i, :], xc[:, h * DH + i, :],
                                           ALU.mult).then_inc(s_dtxp, 1)
                    pool.wait_ge(s_dtxp, (b * HALVES + h + 1) * (DH - 1))

                    def input(n, t, i):
                        pool.wait_ge(s_scan, unit(b, h, n, i) + 1)
                        pool.tensor_tensor(ub[:, i % 2, :], dtx[:, i, :], bn[:, t, :], ALU.mult).then_inc(s_u, 1)

                    pool.wait_ge(s_B[0], b_loads(b, h, 0))
                    for i in range(DH):
                        if i == DH - 1:
                            pool.wait_ge(s_dtx, b * HALVES + h + 1)
                        input(0, 0, i)
                    with pool.Fori(0, NS // 2 - 1) as g:
                        for t in range(2):
                            pool.wait_ge(s_B[1 - t], b_loads(b, h, g + t))
                            for i in range(DH):
                                input(2 * g + (1 + t), 1 - t, i)
                    pool.wait_ge(s_B[1], b_loads(b, h, NS // 2 - 1))
                    for i in range(DH):
                        input(NS - 1, 1, i)
                pool.wait_ge(s_xg, 16 * b + 16)
                after_wait(pool)
                def add_x(tb):
                    pool.wait_ge(s_mf, m_half(b, HALVES, 0) + tb + 3)
                    pool.tensor_tensor(xt[:, tb, :], xt[:, tb, :], gt[:, tb, :], ALU.add).then_inc(s_o, 1)

                for tb in range(TB):
                    add_x(tb)
                    if b + 1 < NB and tb == 2:
                        layer_norm(b + 1)

        @block.scalar
        def _(act):
            give_credits(act, "scalar")
            def layer_norm(b):
                act.wait_ge(s_mv, b * TB + TB)
                act.activation(rs[:, :], mv[:, :, 1], ACT.Sqrt, bias=LN_EPS).then_inc(s_std, 1)
                for tb in range(TB):
                    act.wait_ge(s_tfa, t_use(b, tb) + 1)
                    act.activation(xnT[:, :, tb * P:(tb + 1) * P],
                                   psT[:, tb % 2, :].rearrange("p (k t) -> p k t", k=HK),
                                   ACT.Copy).then_inc(s_tact, 1)

            act.wait_ge(s_const, 32)
            act.activation(negA, negA, ACT.Exp).then_inc(s_negA, 1)
            layer_norm(0)
            for b in range(NB):
                def start_conv(m):
                    act.wait_ge(s_wp, w_use(b, m) + 3)
                    act.wait_ge(s_xc, b * DB + m + 1)
                    act.activation(tmp[:, m % 2, :], psA[:, m % 2, :], ACT.Identity,
                                   bias=hc[:, m, KC:KC + 1], scale=hc[:, m, KC - 1:KC]).then_inc(s_acc, 1)

                act.wait_ge(s_prep, 2)
                act.wait_ge(s_y, b * DB + 1)
                start_conv(0)
                for m in range(DB):
                    act.wait_ge(s_af, a_use(b, m) + 3)
                    act.activation(tmp[:, 2 + m % 2, :], tmp[:, m % 2, :], ACT.Tanh).then_inc(s_thc, 1)
                    for j in range(PT):
                        if m + 1 < DB and j == PT - 1:
                            start_conv(m + 1)
                        it = PT * m + j
                        if b == 0 and it < IT:
                            act.wait_ge(s_lrr, 2 * it + 5)
                            act.dma_start(w_gu[it], wf[:, it % QD, :]).then_inc(s_wst[it % QD], 16)
                v = psM[:, 0, :].rearrange("p (a e) -> p a e", e=E)
                act.wait_ge(s_xp, b + 1)
                act.activation(sq, v, ACT.Square).then_inc(s_sq, 1)
                act.activation(ssm[:, :, :], v, ACT.Copy).then_inc(s_xpr, 1)
                act.wait_ge(s_ms, 2 * b + 2)
                act.activation(ms[:, :, 0:1], ms[:, :, 0:1], ACT.Sqrt, bias=RMS_EPS, scale=1.0 / R).then_inc(s_rms, 1)
                act.activation(ms[:, :, 1:3], ms[:, :, 1:3], ACT.Sqrt, bias=RMS_EPS, scale=1.0 / NS).then_inc(s_rms, 1)
                for t in range(2):
                    act.wait_ge(s_tfa, t_use(b, TB + t) + 1)
                    act.activation(ssT[:, t * 512:(t + 1) * 512], psT[0:E, t, :], ACT.Copy).then_inc(s_tact, 1)

                for h in range(HALVES):
                    def relu_abs(i):
                        k = blk(b, h, i)
                        e, w = soft_tmp(i)
                        v = psA[:, i % 2, :]
                        bias = cc[:, h * DH + i, DTB:DTB + 1]
                        act.wait_ge(s_dtp, k + 1)
                        if i >= 2:
                            act.wait_ge(s_dt, k - 1)
                        act.activation(e, v, ACT.Abs, bias=bias).then_inc(s_abs, 1)
                        act.activation(dt[:, i, :], v, ACT.Relu, bias=bias).then_inc(s_dtr, 1)

                    def one_plus_exp(i):
                        k = blk(b, h, i)
                        e, w = soft_tmp(i)
                        act.wait_ge(s_abs, k + 1)
                        act.activation(e, e, ACT.Exp, scale=-1.0).then_inc(s_e, 1)
                        act.wait_ge(s_e, k + 1)
                        act.activation(w, e, ACT.Identity, bias=1.0).then_inc(s_e1, 1)

                    def log(i):
                        k = blk(b, h, i)
                        e, w = soft_tmp(i)
                        act.wait_ge(s_e1, k + 1)
                        act.wait_ge(s_nd, k + 1)
                        act.activation(w, w, ACT.Ln).then_inc(s_ln, 1)

                    def decay(n, i):
                        act.wait_ge(s_scan, unit(b, h, n, i) + 1)
                        act.activation(psA[:, i % 2, :], dt[:, i, :], ACT.Exp,
                                       scale=negA[:, h * DH + i, bass.ds(n, 1)]).then_inc(s_a, 1)

                    def tanh_gate(n, t):
                        act.wait_ge(s_fg, fg_use(b, h, n) + 1)
                        act.activation(th[0:IM, t, :], psM[0:IM, 0, :], ACT.Tanh, scale=0.5).then_inc(s_th, 1)

                    def ahead(n):
                        tanh_gate(n, n % 2)

                    def tanh_late(kind, i, c):
                        t = c if kind == "z" else i % 2
                        if kind == "d":
                            act.wait_ge(s_fd, b * TB + h * JD + i + 1)
                        elif c == 0:
                            act.wait_ge(s_fg, fg_use(b, h, IT + i) + 1)
                        else:
                            act.wait_ge(s_wp, w_use(b, w_half(h, IT + i)) + 3)
                        if kind == "z" and i == 0:
                            n = IT - 1 - (IT - 1 - c) % 2
                            act.wait_ge(s_mf, m_half(b, h, 2 * n + 1) + 3)
                        else:
                            act.wait_ge(s_ths[t], th_stored(b, h, (i if kind == "z" else DH + i // 2) - 1))
                        act.activation(th[:, t, :], psM[:, t, :], ACT.Tanh, scale=0.5).then_inc(s_th, 1)

                    for t in range(2):
                        act.wait_ge(s_ths[t], th_stored(b, h, -1))
                    for i in range(DH):
                        if i == 0 and h == 0:
                            ahead(0)
                        relu_abs(i)
                        if i == 3:
                            ahead(2 - h)
                        if i:
                            log(i - 1)
                        one_plus_exp(i)
                        if i == 1:
                            ahead(1 - h)
                    act.wait_ge(s_dtr, blk(b, h, DH))
                    for i in range(DH):
                        act.wait_ge(s_dt, blk(b, h, i) + 1)
                        decay(0, i)
                        if i == 0:
                            log(DH - 1)
                        if i == 1 and h:
                            ahead(2)
                    with act.Fori(0, LATE // 2) as g:
                        for t in range(2):
                            n = 2 * g + t
                            for i in range(DH):
                                decay(n + 1, i)
                                if i == 2:
                                    tanh_gate(n + FILL, (FILL + t) % 2)
                    for p in range(QUARTERS):
                        if p + 4 < QUARTERS:
                            decay(LATE + 1 + p // 4, p % 4)
                        if p:
                            for what in ends(p - 1):
                                tanh_late(*what)
                    for what in ends(QUARTERS - 1):
                        tanh_late(*what)
                if b + 1 < NB:
                    layer_norm(b + 1)

        @block.tensor
        def _(pe):
            give_credits(pe, "tensor")
            def layer_norm(b, tb):
                pe.wait_ge(s_xn, b * TB + tb + 1)
                pe.wait_ge(s_tact, t_use(b, tb) + 1)
                for k in range(HK):
                    mm = pe.transpose(psT[:, tb % 2, k * P:(k + 1) * P], yT[:, tb, k * P:(k + 1) * P], ident[:, :])
                mm.then_inc(s_tfa, 1)

            def in_proj(t, dst):
                for c in range(2):
                    for k in range(HK):
                        mm = pe.matmul(psA[:, dst, c * 512:(c + 1) * 512], w_is[:, t, k, :],
                                       xnT[:, k, c * 512:(c + 1) * 512], start=(k == 0), stop=(k == HK - 1))
                return mm

            def low_rank(use):
                pe.wait_ge(s_lrr, use + 1)
                bank = lr_bank(use)
                if use < 2 * IT:
                    for k in range(HK):
                        at = use % 2 * H + k * P
                        mm = pe.matmul(bank[:, k * IM:(k + 1) * IM], at_gu[:, at:at + P],
                                       b_gu[:, use * IM:(use + 1) * IM], start=True, stop=True)
                else:
                    at = (use - 2 * IT) * IM
                    mm = pe.matmul(bank[0:IM, :], at_dn[:, at:at + IM], b_dn, start=True, stop=True)
                mm.then_inc(s_lr, 1)

            def gate_up(b, h, n, t, q, land):
                gu = q // 2
                if q == 0:
                    pe.wait_ge(s_w[t], land)
                if q % 2 == 0:
                    pe.wait_ge(s_mf, m_half(b, h, 2 * n + gu) + 1)
                for k in range(2 * (q % 2), 2 * (q % 2) + 2):
                    at = (gu * HK + k) * IM
                    mm = pe.matmul(psM[0:IM, gu, :], w_ts[:, t, at:at + IM],
                                   xnT[:, k, h * CH:(h + 1) * CH], start=(k == 0), stop=(k == HK - 1))
                if q % 2 == 1:
                    mm.then_inc(s_fg if gu == 0 else s_wp, 1)

            pe.wait_ge(s_ident, 2)
            for tb in range(TB):
                layer_norm(0, tb)
            for b in range(NB):
                pe.wait_ge(s_tact, t_use(b, TB) + 2)

                def x_part(m):
                    pe.wait_ge(s_w[m % 2], landed(b, m))
                    pe.wait_ge(s_af, a_use(b, m) + 1)
                    in_proj(m % 2, m % 2).then_inc(s_wp, 1)

                def x_proj(k):
                    pe.wait_ge(s_xc, b * DB + k + 3)
                    for tb in range(TB):
                        mm = pe.matmul(psM[:, 0, tb * E:(tb + 1) * E], xc[:, k, tb * P:(tb + 1) * P], wx[:, k, :],
                                       start=(k == 0 and tb == 0), stop=(k == DB - 1 and tb == TB - 1))
                    return mm

                x_part(0)
                if b == 0:
                    pe.wait_ge(s_fc, 96)
                pe.wait_ge(s_wx, 16 * b + 16)
                pe.wait_ge(s_mf, b * M_USES + 2)
                if b == 0:
                    for use in range(3):
                        low_rank(use)
                for m in range(DB):
                    if m + 1 < DB:
                        x_part(m + 1)
                    if b == 0:
                        for use in range(lr_uses(m) + 3, min(lr_uses(m + 1) + 3, LR_USES)):
                            low_rank(use)
                    if m > 0:
                        x_proj(m - 1)
                x_proj(DB - 1).then_inc(s_xp, 1)
                if b == 0:
                    pe.wait_ge(s_lrr, LR_USES + 3)
                pe.wait_ge(s_xpr, b + 1)
                for q in range(2):
                    gate_up(b, 0, 0, 0, q, landed(b, w_half(0, 0)))
                pe.wait_ge(s_sn, b + 1)
                for t in range(2):
                    pe.wait_ge(s_tact, t_use(b, TB + t) + 1)
                    after_wait(pe)
                    for a in range(TB // 2):
                        mm = pe.transpose(psT[0:E, t, a * P:(a + 1) * P], ssm[:, t * TB // 2 + a, :], ident[:, :])
                    mm.then_inc(s_tfa, 1)
                pe.wait_ge(s_tact, t_use(b, TB + 2) + 2)

                for h in range(HALVES + 1):
                    def dt_proj(i):
                        if i == 0:
                            pe.wait_ge(s_wdt, b * 48 + 16 + 32 * h)
                            pe.wait_ge(s_af, a_use(b, DB) + 2)
                            if h:
                                pe.wait_ge(s_scan, unit(b, h, 0, 0) + 2)
                        if i > 1:
                            pe.wait_ge(s_dtr, blk(b, h, i - 1))
                        m = (h * DH + i) * P
                        for c in range(2):
                            mm = pe.matmul(psA[:, i % 2, c * 512:(c + 1) * 512], wdt[:, m:m + P],
                                           ssT[0:R, c * 512:(c + 1) * 512], start=True, stop=True)
                        mm.then_inc(s_dtp, 1)

                    def turn_back(i):
                        pe.wait_ge(s_tdve, t_group(b, h, 0, 0) + 2)
                        pe.wait_ge(s_ybr, blk(b, h - 1, i) + 1)
                        for tb in range(TB):
                            mm = pe.transpose(psT[:, tb // 4, tb % 4 * P:(tb % 4 + 1) * P],
                                              yT[:, tb, i * P:(i + 1) * P], ident[:, :])
                        mm.then_inc(s_yb, 1)

                    def turn(n, t, tb):
                        if tb == 0:
                            pe.wait_ge(s_scan, unit(b, h, n, DH) + 2)
                            if h:
                                pe.wait_ge(s_ybr, blk(b, h, 0) + 1)
                        pe.wait_ge(s_tdve, t_group(b, h, n, tb) + 1)
                        for i in range(DH):
                            mm = pe.transpose(psT[:, tb % 2, i * P:(i + 1) * P],
                                              hb[:, t * DH + i, tb * P:(tb + 1) * P], ident[:, :])
                        mm.then_inc(s_tfd, 1)

                    def z_part(i, step):
                        off = w_half(h, IT + i)
                        c, k = divmod(step, HK)
                        if step == 0:
                            pe.wait_ge(s_w[off % 2], landed(b, off))
                        if k == 0:
                            pe.wait_ge(s_mf, m_late(b, h, "z", i, c) + 1)
                        mm = pe.matmul(psM[:, c, :], w_is[:, off % 2, k, :], xnT[:, k, c * 512:(c + 1) * 512],
                                       start=(k == 0), stop=(k == HK - 1))
                        if k == HK - 1:
                            mm.then_inc(s_fg if c == 0 else s_wp, 1)

                    def down(j, k):
                        if k == 0:
                            pe.wait_ge(s_mf, m_late(b, h, "d", j, 0) + 1)
                        if k == IT - 1 and j == 0:
                            pe.wait_ge(s_mf, m_half(b, h, 2 * IT - 1) + 3)
                        mm = pe.matmul(psM[:, j % 2, :], hid[0:IM, k, j * P:(j + 1) * P], w_dn[0:IM, k, :],
                                       start=(k == 0), stop=(k == IT - 1))
                        if k == IT - 1:
                            mm.then_inc(s_fd, 1)

                    if h == HALVES:
                        break

                    def ahead(n):
                        for q in range(4):
                            gate_up(b, h, n, w_half(h, n) % 2, q, landed(b, w_half(h, n)))

                    dt_proj(0)
                    dt_proj(1)
                    if h:
                        turn_back(0)
                    else:
                        for q in range(2, 4):
                            gate_up(b, 0, 0, 0, q, landed(b, w_half(0, 0)))
                    dt_proj(2)
                    if h:
                        turn_back(1)
                    ahead(1 - h)
                    dt_proj(3)
                    if h:
                        turn_back(2)
                    ahead(2 - h)
                    if h:
                        turn_back(3)
                    for n in range(3 - h, FILL):
                        ahead(n)
                    with pe.Fori(0, LATE // 2) as g:
                        for t in range(2):
                            for q in range(4):
                                turn(2 * g + t, t, 2 * q)
                                turn(2 * g + t, t, 2 * q + 1)
                                gate_up(b, h, 2 * g + (FILL + t), (w_half(h, FILL) + t) % 2, q,
                                        landed(b, w_half(h, FILL) + t) + 16 * g)
                    for p in range(QUARTERS):
                        n, q = LATE + p // 4, p % 4
                        turn(n, n % 2, 2 * q)
                        turn(n, n % 2, 2 * q + 1)
                        for kind, i, step in steps_of(p):
                            if kind == "z":
                                z_part(i, step)
                            else:
                                down(i, step)
                def out_part(tb, ks):
                    if ks[0] == 0:
                        pe.wait_ge(s_mf, m_half(b, HALVES, 0) + tb + 1)
                    for k in ks:
                        if tb == 0:
                            pe.wait_ge(s_y, b * DB + k + 2)
                        mm = pe.matmul(psM[:, tb % 2, :], xc[:, k, tb * P:(tb + 1) * P], w_o[:, k, :],
                                       start=(k == 0), stop=(k == DB - 1))
                    if ks[-1] == DB - 1:
                        mm.then_inc(s_sp, 1)

                pe.wait_ge(s_wo, 16 * b + 16)
                for i in range(DH):
                    turn_back(i)
                    out_part(i // 2, range(i % 2 * 2, i % 2 * 2 + 2))
                for tb in range(2):
                    out_part(tb, range(DH, DB))
                if b + 1 < NB:
                    pe.wait_ge(s_ybr, blk(b, HALVES, 0) + 1)
                for tb in range(2, TB):
                    out_part(tb, range(DB))
                    if b + 1 < NB and tb >= TB // 2:
                        layer_norm(b + 1, 2 * tb - TB)
                        layer_norm(b + 1, 2 * tb - TB + 1)

        @block.vector
        def _(dve):
            give_credits(dve, "vector")

            def stt(out, in0, scalar, in1, op0, op1):
                return dve.scalar_tensor_tensor(out=out, in0=in0, scalar=scalar, in1=in1, op0=op0, op1=op1)

            psT_row = psT[:, :, :].rearrange("p a c -> p (a c)")

            def statistics(b):
                dve.wait_ge(s_x, 16 * b + 16)
                for tb in range(TB):
                    dve.bn_stats(st[:, tb, :], yT[:, tb, :]).then_inc(s_st, 1)
                for tb in range(TB):
                    dve.wait_ge(s_st, b * TB + tb + 1)
                    dve.bn_aggr(mv[:, tb, :], st[:, tb, :]).then_inc(s_mv, 1)

            def scale_shift(b):
                dve.wait_ge(s_std, b + 1)
                dve.reciprocal(rs[:, :], rs[:, :]).then_inc(s_rstd, 1)
                dve.wait_ge(s_rstd, b + 1)
                stt(nm[:, :], mv[:, :, 0], -1.0, rs[:, :], ALU.mult, ALU.mult).then_inc(s_nm, 1)

            def ffn_weights(it):
                t = it % QD
                dve.wait_ge(s_q[t], 16 * (it // QD) + 16)
                if it < IT:
                    dve.wait_ge(s_wst[t], 16 * (it // QD) + 16)
                    for gu in range(2):
                        sl = slice(gu * HK * IM, (gu + 1) * HK * IM)
                        at = (2 * it + gu) * IM
                        scale = scales[:, at:at + IM].rearrange("p (k i) -> p k i", k=1).to_broadcast([P, HK, IM])
                        ins = stt(wf[:, t, sl].rearrange("p (k i) -> p k i", k=HK),
                                  qs[t][:, sl].rearrange("p (k i) -> p k i", k=HK), -Q_ZERO, scale, ALU.add, ALU.mult)
                    ins.then_inc(s_deq, 1)
                    dve.wait_ge(s_deq, it + QD + 1)
                    for gu in range(2):
                        use = 2 * it + gu
                        w = wf[:, t, gu * HK * IM:(gu + 1) * HK * IM]
                        dve.wait_ge(s_lr, use + 1)
                        stt(w, lr_bank(use)[:, 0:HK * IM], LR_SCALE, w, ALU.mult, ALU.add).then_inc(s_lrr, 1)
                else:
                    use = IT + it
                    w = w_dn[0:IM, it - IT, :]
                    stt(w, qs[t][0:IM, 0:H], -Q_ZERO, scales[0:IM, 2 * IT * IM:], ALU.add, ALU.mult).then_inc(s_deq, 1)
                    dve.wait_ge(s_deq, it + QD + 1)
                    dve.wait_ge(s_lr, use + 1)
                    stt(w, lr_bank(use)[0:IM, :], LR_SCALE, w, ALU.mult, ALU.add).then_inc(s_lrr, 1)

            psT_row = psT[:, :, :].rearrange("p a c -> p (a c)")
            statistics(0)
            dve.wait_ge(s_const, 32)
            dve.tensor_scalar(hc, hc, 0.5, None, ALU.mult).then_inc(s_prep, 1)
            dve.wait_ge(s_negA, 1)
            dve.tensor_scalar(negA, negA, -1.0, None, ALU.mult).then_inc(s_prep, 1)
            scale_shift(0)
            dve.wait_ge(s_fc, 96)
            dve.tensor_scalar(scales, scales, Q_STEP, None, ALU.mult).then_inc(s_scl, 1)
            dve.wait_ge(s_scl, 1)

            for b in range(NB):
                def conv(m, t):
                    dve.wait_ge(s_acc, b * DB + m + 1)
                    for k in range(KC - 2, -1, -1):
                        lag = KC - 1 - k
                        if k < KC - 2:
                            dve.wait_ge(s_tap, b * (2 * DB) + 2 * m + lag - 1)
                        ins = stt(tmp[:, t, lag:L], psA[:, t, 0:L - lag], hc[:, m, k:k + 1], tmp[:, t, lag:L],
                                  ALU.mult, ALU.add)
                        ins.then_inc(s_tap if k else s_af, 1)

                def conv_silu(m, t):
                    dve.wait_ge(s_thc, b * DB + m + 1)
                    stt(xc[:, m, :], tmp[:, 2 + t, :], 1.0, tmp[:, t, :], ALU.add, ALU.mult).then_inc(s_xc, 1)

                for m in range(DB):
                    conv(m, m % 2)
                    if b == 0:
                        if PT * m < 2 * IT:
                            ffn_weights(PT * m)
                    conv_silu(m, m % 2)
                    if b == 0:
                        for it in range(PT * m + 1, min(PT * (m + 1), 2 * IT)):
                            ffn_weights(it)
                dve.wait_ge(s_sq, b + 1)
                dve.tensor_reduce(ms[:, :, 0:1], sq[:, :, 0:R], AX.X, ALU.add).then_inc(s_ms, 1)
                dve.tensor_reduce(ms[:, :, 1:3], sq[:, :, R:E].rearrange("p a (g n) -> p a g n", g=2), AX.X,
                                  ALU.add).then_inc(s_ms, 1)
                dve.wait_ge(s_rms, 2 * b + 2)
                dve.reciprocal(ms[:, :, :], ms[:, :, :]).then_inc(s_rinv, 1)
                dve.wait_ge(s_rinv, b + 1)
                dve.wait_ge(s_xpr, b + 1)
                for g, (lo, hi) in enumerate([(0, R), (R, R + NS), (R + NS, E)]):
                    dve.tensor_tensor(ssm[:, :, lo:hi], ssm[:, :, lo:hi],
                                      ms[:, :, g:g + 1].to_broadcast([P, TB, hi - lo]), ALU.mult).then_inc(s_sn1, 1)
                dve.wait_ge(s_sn1, 3 * b + 3)
                dve.tensor_tensor(ssm[:, :, :], ssm[:, :, :],
                                  lnw[:, :].rearrange("p (a e) -> p a e", a=1).to_broadcast([P, TB, E]), ALU.mult
                                  ).then_inc(s_sn, 1)

                for h in range(HALVES + 1):
                    def lost(i):
                        k = blk(b, h, i)
                        e, w = soft_tmp(i)
                        dve.wait_ge(s_e1, k + 1)
                        stt(e, w, -1.0, e, ALU.add, ALU.subtract).then_inc(s_nd, 1)

                    def softplus(i):
                        k = blk(b, h, i)
                        e, w = soft_tmp(i)
                        dve.wait_ge(s_nd, k + 1)
                        dve.wait_ge(s_ln, k + 1)
                        dve.tensor_tensor(e, w, e, ALU.subtract).then_inc(s_rl, 1)
                        dve.wait_ge(s_rl, k + 1)
                        dve.tensor_tensor(dt[:, i, :], dt[:, i, :], e, ALU.add).then_inc(s_dt, 1)

                    def finish_y(i):
                        k, m = blk(b, h - 1, i), (h - 1) * DH + i
                        dve.wait_ge(s_yb, k + 1)
                        stt(xc[:, m, :], xc[:, m, :], cc[:, m, DP:DP + 1], psT_row, ALU.mult, ALU.add).then_inc(s_ybr, 1)
                        dve.wait_ge(s_zl, 16 * blk(b, h, 0))
                        dve.wait_ge(s_ybr, k + 2)
                        stt(xc[:, m, :], xc[:, m, :], 0.5, tmp[:, i, :], ALU.mult, ALU.mult).then_inc(s_y, 1)

                    def scan(n, t, i):
                        dve.wait_ge(s_a, unit(b, h, n, i) + 1)
                        dve.wait_ge(s_u, unit(b, h, n, i) + 9)
                        dve.tensor_tensor_scan(hb[:, t * DH + i, :], psA[:, i % 2, :], ub[:, i % 2, :], 0.0,
                                               ALU.mult, ALU.add).then_inc(s_scan, 1)

                    def add_y(n, tb, first):
                        dve.wait_ge(s_tfd, t_group(b, h, n, tb) + 1)
                        if not first:
                            dve.wait_ge(s_tdve, t_group(b, h, n - 1, tb) + 3)
                            stt(yT[:, tb, :], psT[:, tb % 2, :], ssm[:, tb, bass.ds(n + (R + NS), 1)], yT[:, tb, :],
                                ALU.mult, ALU.add).then_inc(s_tdve, 1)
                        else:
                            dve.tensor_scalar(yT[:, tb, :], psT[:, tb % 2, :], ssm[:, tb, R + NS:R + NS + 1], None,
                                              ALU.mult).then_inc(s_tdve, 1)

                    def silu_gate(n, t):
                        dve.wait_ge(s_th, (b * HALVES + h) * (IT + 2 * DH + JD) + n + 1)
                        stt(th[0:IM, t, :], th[0:IM, t, :], 1.0, psM[0:IM, 0, :], ALU.add, ALU.mult).then_inc(s_mf, 1)

                    def hidden(n, t):
                        dve.wait_ge(s_wp, w_use(b, n + w_half(h, 0)) + 3)
                        dve.wait_ge(s_mf, m_half(b, h, 2 * n) + 3)
                        stt(hid[0:IM, n, :], th[0:IM, t, :], 0.5, psM[0:IM, 1, :], ALU.mult, ALU.mult).then_inc(s_mf, 1)

                    def silu_late(kind, i, c):
                        t = c if kind == "z" else i % 2
                        dve.wait_ge(s_th, th_done(b, h, kind, i, c))
                        stt(th[:, t, :], th[:, t, :], 1.0, psM[:, t, :], ALU.add, ALU.mult).then_inc(s_mf, 1)

                    def slot(n, t, first=False, gate=None, up=None):
                        for i in range(DH):
                            scan(n + 1, 1 - t, i)
                            add_y(n, 2 * i, first)
                            if i == DH - 1:
                                silu_gate(gate, (FILL + t) % 2)
                            add_y(n, 2 * i + 1, first)
                            if i == 0:
                                hidden(up, (FILL + t - 1) % 2)

                    if h == HALVES:
                        for i in range(DH):
                            finish_y(i)
                        break
                    for i in range(DH):
                        if i == 0 and h == 0:
                            silu_gate(0, 0)
                        if i == 3:
                            silu_gate(2 - h, h)
                        lost(i)
                        if i == 0 and h == 0:
                            dve.wait_ge(s_out, b * (TB * 16) + 16)
                            hidden(0, 0)
                        if h:
                            finish_y(i)
                        if i == 1:
                            silu_gate(1 - h, 1 - h)
                        softplus(i)
                        if i == 1:
                            hidden(1 - h, 1 - h)
                    dve.wait_ge(s_dt, blk(b, h, DH))
                    dve.tensor_tensor(dtx[:, DH - 1, :], dt[:, DH - 1, :], xc[:, h * DH + DH - 1, :],
                                      ALU.mult).then_inc(s_dtx, 1)
                    scan(0, 0, 0)
                    if h:
                        hidden(1, 1)
                    scan(0, 0, 1)
                    if h:
                        silu_gate(2, 0)
                    scan(0, 0, 2)
                    scan(0, 0, 3)
                    if h == 0:
                        dve.wait_ge(s_tfa, t_use(b, TB))
                    else:
                        dve.wait_ge(s_yb, blk(b, h, 0))
                    slot(0, 0, first=True, gate=FILL, up=FILL - 1)
                    with dve.Fori(0, LATE // 2 - 1) as g:
                        slot(2 * g + 1, 1, gate=2 * g + (FILL + 1), up=2 * g + FILL)
                        slot(2 * g + 2, 0, gate=2 * g + (FILL + 2), up=2 * g + (FILL + 1))
                    slot(LATE - 1, 1, gate=IT - 1, up=IT - 2)
                    for p in range(QUARTERS):
                        n, q = LATE + p // 4, p % 4
                        if n + 1 < NS:
                            scan(n + 1, 1 - n % 2, q)
                        add_y(n, 2 * q, False)
                        if p:
                            for what in ends(p - 1):
                                silu_late(*what)
                        add_y(n, 2 * q + 1, False)
                        if p == 0:
                            hidden(IT - 1, (IT - 1) % 2)
                    for what in ends(QUARTERS - 1):
                        silu_late(*what)
                dve.wait_ge(s_gl, 16 * b + 16)
                for tb in range(TB):
                    dve.wait_ge(s_sp, b * TB + tb + 1)
                    stt(gt[:, tb, :], psM[:, tb % 2, :], 0.5, gt[:, tb, :], ALU.mult, ALU.mult).then_inc(s_mf, 1)
                    if b + 1 < NB and tb == 2:
                        statistics(b + 1)
                    if b + 1 < NB and tb == 3:
                        scale_shift(b + 1)


def kernel(**inputs):
    import concourse.bacc as bacc
    from concourse.bass_utils import run_bass_kernel_spmd

    def arr(name):
        return np.asarray(inputs[name])

    def pad(a, axis):
        width = [(0, 0)] * a.ndim
        width[axis] = (0, IT * IM - I)
        return np.pad(a, width)

    def per_channel(a):
        return a.reshape(DB, P, -1).transpose(1, 0, 2)

    def ffn_in(q):
        return pad(q, 0).reshape(IT, IM, HK, P).transpose(0, 3, 2, 1)

    A, F = "L0_attn_", "L0_ffn_"
    gu = ("gate", "up")
    data = {
        "x": arr(A + "hidden_states"),
        "w_in": arr(A + "in_proj_w").reshape(HK, P, 2 * DB, P).transpose(2, 1, 0, 3),
        "chan": np.concatenate([per_channel(arr(A + n)) for n in ("conv_w", "conv_b", "dt_bias", "D_param", "A_log")], 2),
        "w_x": per_channel(arr(A + "x_proj_w").T),
        "w_dt": arr(A + "dt_proj_w").T,
        "ln_w": np.concatenate([arr(A + n) for n in ("dt_ln_w", "B_ln_w", "C_ln_w")])[None],
        "w_out": per_channel(arr(A + "out_proj_w").T),
        "gu_q": np.stack([ffn_in(arr(F + n + "_q")) for n in gu], 2).reshape(IT, P, 2 * HK * IM),
        "gu_s": np.stack([pad(arr(F + n + "_scale"), 0).reshape(IT, IM) for n in gu], 1).reshape(1, -1),
        "gu_at": np.stack([arr(F + n + "_A").T for n in gu], 1),
        "gu_b": np.stack([pad(arr(F + n + "_B"), 1).reshape(R, IT, IM) for n in gu], 2).reshape(R, -1),
        "dn_q": pad(arr(F + "down_q").T, 0).reshape(IT, IM, H),
        "dn_s": arr(F + "down_scale")[None],
        "dn_at": pad(arr(F + "down_A"), 0).T,
        "dn_b": arr(F + "down_B"),
    }
    data = {f"{n}_dram": np.ascontiguousarray(a) for n, a in data.items()}
    nc = bacc.Bacc("TRN2", target_bir_lowering=False, num_devices=1)
    args = [nc.dram_tensor(n, a.shape, mybir.dt.from_np(a.dtype), kind="ExternalInput").ap() for n, a in data.items()]
    args.append(nc.dram_tensor("out_dram", (NB, L, H), F32, kind="ExternalOutput").ap())
    build(nc, *args)
    r = run_bass_kernel_spmd(nc, [data], core_ids=[0])
    return r.results[0]["out_dram"]
```
